# Optimizing a Trainium2 kernel written in Bass

```python
import numpy as np
import jax
import jax.numpy as jnp

def _softmax(x, axis=-1):
    return jax.nn.softmax(x, axis=axis)
def _gelu(x):
    return jax.nn.gelu(x, approximate=True)
def _silu(x):
    return jax.nn.silu(x)
def _sigmoid(x):
    return jax.nn.sigmoid(x)
def _layernorm(x, axis=-1, eps=1e-5):
    m = jnp.mean(x, axis=axis, keepdims=True)
    v = jnp.var(x, axis=axis, keepdims=True)
    return (x - m) / jnp.sqrt(v + eps)
def _scatter_add(tgt, idx, src, axis=0):
    return tgt.at[idx].add(src)
def _segment_sum(src, seg, n):
    return jax.ops.segment_sum(src, seg, n)

kernel_name = 'mk_conv_preact_d2_conv_nchw48_2c24cf'

def setup_inputs(seed: int = 0):
    np.random.seed(seed)
    _w = jnp.asarray
    def _rec_inputs():
        import jax
        import jax.numpy as jnp
        _gk = jax.random.key(seed)
        x = -0.0002221 + 1 * jax.random.normal(jax.random.fold_in(_gk, 1), (2, 48, 512, 512), jnp.float32)
        return x
    x = _rec_inputs()
    def _L0_conv_setup():
        import jax, jax.numpy as jnp
        import numpy as np
        from jax import lax
        DIM = 48
        HEADS = 8
        NBLK = 4
        DN = ('NCHW', 'OIHW', 'NCHW')
        EPS = 1e-12

        def _to_blocks(t, b, heads, c, h1, w1, N):
            t = t.reshape(b, heads, c, h1, N, w1, N)
            t = t.transpose(0, 1, 2, 4, 6, 3, 5)
            return t.reshape(b, heads, c * N * N, h1 * w1)

        def _from_blocks(t, b, heads, c, h1, w1, N):
            t = t.reshape(b, heads, c, N, N, h1, w1)
            t = t.transpose(0, 1, 2, 5, 3, 6, 4)
            return t.reshape(b, heads * c, h1 * N, w1 * N)
        key = jax.random.key(seed)
        ks = jax.random.split(key, 5)
        return {'x': jax.random.normal(ks[0], (2, DIM, 512, 512), dtype=jnp.float32), 'qkv_w': jax.random.normal(ks[1], (3 * DIM, DIM, 1, 1), dtype=jnp.float32) * 0.05, 'dw_w': jax.random.normal(ks[2], (3 * DIM, 1, 3, 3), dtype=jnp.float32) * 0.05, 'proj_w': jax.random.normal(ks[3], (DIM, DIM, 1, 1), dtype=jnp.float32) * 0.05, 'temperature': jnp.ones((HEADS, 1, 1), dtype=jnp.float32)}
    _L0_conv_all = _L0_conv_setup()
    _L0_conv_in = {k: v for k, v in _L0_conv_all.items() if k in ('qkv_w', 'dw_w', 'proj_w', 'temperature', )}
    del _L0_conv_all

    def _L1_conv_setup():
        import jax, jax.numpy as jnp
        import numpy as np
        B, C, H, W = (32, 48, 64, 128)
        K = 5

        def _conv1d(x, w, b):
            y = jax.lax.conv_general_dilated(x, w, window_strides=(1,), padding=[(2, 2)], dimension_numbers=('NCH', 'OIH', 'NCH'))
            return y + b[None, :, None]
        key = jax.random.key(seed)
        ks = jax.random.split(key, 7)
        s = 0.02
        return {'x': jax.random.normal(ks[0], (B, C, H, W), dtype=jnp.float32), 'down_w': jax.random.normal(ks[1], (C, C, K), dtype=jnp.float32) * s, 'down_b': jax.random.normal(ks[2], (C,), dtype=jnp.float32) * s, 'right_w': jax.random.normal(ks[3], (C, C, K), dtype=jnp.float32) * s, 'right_b': jax.random.normal(ks[4], (C,), dtype=jnp.float32) * s, 'left_w': jax.random.normal(ks[5], (C, C, K), dtype=jnp.float32) * s, 'left_b': jax.random.normal(ks[6], (C,), dtype=jnp.float32) * s}
    _L1_conv_all = _L1_conv_setup()
    _L1_conv_in = {k: v for k, v in _L1_conv_all.items() if k in ('down_w', 'down_b', 'right_w', 'right_b', 'left_w', 'left_b', )}
    del _L1_conv_all

    return {
        "x": x,
        "L0_conv_qkv_w": _L0_conv_in["qkv_w"],
        "L0_conv_dw_w": _L0_conv_in["dw_w"],
        "L0_conv_proj_w": _L0_conv_in["proj_w"],
        "L0_conv_temperature": _L0_conv_in["temperature"],
        "L1_conv_down_w": _L1_conv_in["down_w"],
        "L1_conv_down_b": _L1_conv_in["down_b"],
        "L1_conv_right_w": _L1_conv_in["right_w"],
        "L1_conv_right_b": _L1_conv_in["right_b"],
        "L1_conv_left_w": _L1_conv_in["left_w"],
        "L1_conv_left_b": _L1_conv_in["left_b"],
    }

def reference(x, L0_conv_qkv_w, L0_conv_dw_w, L0_conv_proj_w, L0_conv_temperature, L1_conv_down_w, L1_conv_down_b, L1_conv_right_w, L1_conv_right_b, L1_conv_left_w, L1_conv_left_b):
    import jax
    import jax.numpy as jnp
    def _L0_conv_ref(x, qkv_w, dw_w, proj_w, temperature):
        import jax, jax.numpy as jnp
        import numpy as np
        from jax import lax
        DIM = 48
        HEADS = 8
        NBLK = 4
        DN = ('NCHW', 'OIHW', 'NCHW')
        EPS = 1e-12

        def _to_blocks(t, b, heads, c, h1, w1, N):
            t = t.reshape(b, heads, c, h1, N, w1, N)
            t = t.transpose(0, 1, 2, 4, 6, 3, 5)
            return t.reshape(b, heads, c * N * N, h1 * w1)

        def _from_blocks(t, b, heads, c, h1, w1, N):
            t = t.reshape(b, heads, c, N, N, h1, w1)
            t = t.transpose(0, 1, 2, 5, 3, 6, 4)
            return t.reshape(b, heads * c, h1 * N, w1 * N)
        b, _, h, w = x.shape
        N = NBLK
        h_pad = -h % N
        w_pad = -w % N
        if h_pad or w_pad:
            x = jnp.pad(x, ((0, 0), (0, 0), (0, h_pad), (0, w_pad)), mode='reflect')
        h_after, w_after = (h + h_pad, w + w_pad)
        h1, w1 = (h_after // N, w_after // N)
        qkv = lax.conv_general_dilated(x, qkv_w, (1, 1), 'VALID', dimension_numbers=DN)
        qkv = lax.conv_general_dilated(qkv, dw_w, (1, 1), ((1, 1), (1, 1)), dimension_numbers=DN, feature_group_count=3 * DIM)
        q, k, v = jnp.split(qkv, 3, axis=1)
        c = DIM // HEADS
        q = _to_blocks(q, b, HEADS, c, h1, w1, N)
        k = _to_blocks(k, b, HEADS, c, h1, w1, N)
        v = _to_blocks(v, b, HEADS, c, h1, w1, N)
        q = q / jnp.maximum(jnp.linalg.norm(q, axis=-1, keepdims=True), EPS)
        k = k / jnp.maximum(jnp.linalg.norm(k, axis=-1, keepdims=True), EPS)
        attn = jnp.einsum('bhcn,bhdn->bhcd', q, k) * temperature
        attn = jax.nn.softmax(attn, axis=-1)
        out = jnp.einsum('bhcd,bhdn->bhcn', attn, v)
        out = _from_blocks(out, b, HEADS, c, h1, w1, N)
        out = lax.conv_general_dilated(out, proj_w, (1, 1), 'VALID', dimension_numbers=DN)
        return out[:, :, :h, :w]

    def _L1_conv_ref(x, down_w, down_b, right_w, right_b, left_w, left_b):
        import jax, jax.numpy as jnp
        import numpy as np
        B, C, H, W = (32, 48, 64, 128)
        K = 5

        def _conv1d(x, w, b):
            y = jax.lax.conv_general_dilated(x, w, window_strides=(1,), padding=[(2, 2)], dimension_numbers=('NCH', 'OIH', 'NCH'))
            return y + b[None, :, None]
        Bb, Cc, Hh, Ww = x.shape

        def step(w, b):

            def f(carry, inp):
                nxt = inp + _conv1d(carry, w, b)
                return (nxt, nxt)
            return f
        xs = jnp.moveaxis(x, 2, 0)
        d0 = xs[0]
        _, d_rest = jax.lax.scan(step(down_w, down_b), d0, xs[1:])
        D = jnp.concatenate([d0[None], d_rest], 0)
        seq = jnp.concatenate([D[Hh - 3::-1], D[Hh - 1:Hh]], 0)
        u0 = D[Hh - 1]
        _, u_rest = jax.lax.scan(step(down_w, down_b), u0, seq)
        U = jnp.concatenate([u0[None], u_rest], 0)[::-1]
        ws = jnp.moveaxis(jnp.moveaxis(U, 0, 2), 3, 0)
        r0 = ws[0]
        _, r_rest = jax.lax.scan(step(right_w, right_b), r0, ws[1:])
        R = jnp.concatenate([r0[None], r_rest], 0)
        l0 = R[Ww - 1]
        _, l_rest = jax.lax.scan(step(left_w, left_b), l0, R[Ww - 2::-1])
        L = jnp.concatenate([l0[None], l_rest], 0)[::-1]
        return jnp.moveaxis(L, 0, 3)

    def _gn(v, G=16, eps=1e-5):
        B_, C_, H_, W_ = v.shape
        g = v.reshape(B_, G, C_ // G, H_, W_)
        m = jnp.mean(g, axis=(2, 3, 4), keepdims=True)
        s = jnp.var(g, axis=(2, 3, 4), keepdims=True)
        return ((g - m) / jnp.sqrt(s + eps)).reshape(v.shape)

    def _ln_c(v, eps=1e-6):
        m = jnp.mean(v, axis=1, keepdims=True)
        s = jnp.var(v, axis=1, keepdims=True)
        return (v - m) / jnp.sqrt(s + eps)

    def _ln_t(v, eps=1e-5):
        m = jnp.mean(v, axis=-1, keepdims=True)
        s = jnp.var(v, axis=-1, keepdims=True)
        return (v - m) / jnp.sqrt(s + eps)

    def _to_tokens(v):
        B_, C_, H_, W_ = v.shape
        return v.reshape(B_, C_, H_ * W_).transpose(0, 2, 1)
    def _from_tokens(t, like):
        B_, C_, H_, W_ = like.shape
        return t.transpose(0, 2, 1).reshape(B_, C_, H_, W_)

    x = x + _L0_conv_ref(_gn(x), L0_conv_qkv_w, L0_conv_dw_w, L0_conv_proj_w, L0_conv_temperature)
    x = x + _L1_conv_ref(_gn(x), L1_conv_down_w, L1_conv_down_b, L1_conv_right_w, L1_conv_right_b, L1_conv_left_w, L1_conv_left_b)
    return x


_drawn_inputs = setup_inputs


def setup_inputs(seed=0):
    import zlib

    import numpy as np

    out = dict(_drawn_inputs(seed))
    spreads = {'L0_conv_temperature': (1.0, 0.6)}
    factors = {'L0_conv_qkv_w': 8.0,
     'L0_conv_dw_w': 8.0,
     'L0_conv_proj_w': 8.0,
     'L1_conv_right_b': 4.413,
     'L1_conv_left_b': 3.663,
     'L1_conv_down_b': 3.069}
    for name, (base, spread) in spreads.items():
        noise = np.random.default_rng([zlib.crc32(name.encode()), seed]).standard_normal(out[name].shape)
        drawn = base * np.exp(spread * noise) if base else spread * noise
        out[name] = jnp.asarray(drawn.astype(out[name].dtype))
    for name, factor in factors.items():
        out[name] = (out[name] * factor).astype(out[name].dtype)
    return out
```

```python
from contextlib import ExitStack

import concourse.bass as bass
from concourse import mybir

F32 = mybir.dt.float32
ALU = mybir.AluOpType
ACT = mybir.ActivationFunctionType
AX = mybir.AxisListType

B, C, H, W = 2, 48, 512, 512
HEADS = 8
HC = C // HEADS
N = 4
TOK = W // N
HD = HC * N * N
ODD = 64
PP = ODD + C
T = 16
G = H // T
NP = T // 2
NQ = NP + 1
NB = T // N
W2 = W // 2
K = 5
GN_EPS = 1e-5
GROUP = C // 16
CFG = 4


def flat(ap):
    return ap.rearrange("p a b -> p (a b)")


def program(nc, x, wqk, wv, dwqk, dwv, projT, temp, down_w, down_b, right_w, right_b, left_w, left_b,
            g96, gsel, g112, ident, out):
    def dram(name, shape):
        return nc.dram_tensor(name, shape, F32).ap()

    x1_scan = dram("x1_scan", (G, PP, T, B, W2))
    x1_rows = dram("x1_rows", (B, G, PP, NP, W))
    mixers = dram("mixers", (B, N * N, HEADS, HC, N * N * C))
    d_rows = dram("d_rows", (G, PP, T, B, W2))
    u_cols = dram("u_cols", (G, PP, B, H // 2, T))
    r_cols = dram("r_cols", (G, PP, T, B, H // 2))
    l_cols = dram("l_cols", (G, PP, B, H // 2, T))

    with ExitStack() as whole:
        def sem(name):
            return whole.enter_context(nc.semaphore(name))

        def keep(name, shape):
            return whole.enter_context(nc.sbuf_tensor(name, shape, F32))

        wqk_dense = keep("wqk_dense", [PP, CFG, 3, 2 * C])
        wv_pair = keep("wv_pair", [PP, 2, 3, PP])
        gn0_scale = keep("gn0_scale", [PP, B])
        gn0_bias = keep("gn0_bias", [PP, B])
        top_scale = keep("top_scale", [PP, B, G])
        top_bias = keep("top_bias", [PP, B, G])
        end_scale = keep("end_scale", [PP, B, G])
        end_bias = keep("end_bias", [PP, B, G])
        x1_stats = keep("x1_stats", [PP, B, G * NP, 6])
        gn1_scale = keep("gn1_scale", [PP, B])
        gn1_bias = keep("gn1_bias", [PP, B])
        g112_sb = keep("g112_sb", [PP, PP])

        setup_and_stats(nc, sem, x, wqk, wv, dwqk, dwv, g96, gsel, g112, wqk_dense, wv_pair, g112_sb,
                        gn0_scale, gn0_bias, top_scale, top_bias, end_scale, end_bias)
        norm0 = (gn0_scale, gn0_bias, top_scale, top_bias, end_scale, end_bias)
        attention(nc, sem, x, wqk_dense, norm0, projT, temp, ident, mixers)
        for b in range(B):
            mix_values(nc, sem, b, x, wv_pair, norm0, mixers, x1_scan, x1_rows, x1_stats)
        combine_stats(nc, sem, x1_stats, g112_sb, gn1_scale, gn1_bias)
        scan(nc, sem, "down", down_w, down_b, x1_scan, d_rows, gn1_scale, gn1_bias)
        scan(nc, sem, "up", down_w, down_b, d_rows, u_cols, None, None)
        scan(nc, sem, "right", right_w, right_b, u_cols, r_cols, None, None)
        scan(nc, sem, "left", left_w, left_b, r_cols, l_cols, None, None)
        final_sum(nc, sem, x1_rows, l_cols, out)


def inverse_root(nc, link, out, value, root):
    link(nc.vector.reciprocal(out, root))
    link(nc.vector.tensor_tensor(out, out, value, ALU.mult))
    link(nc.vector.tensor_tensor(out, out, root, ALU.add))
    link(nc.vector.tensor_scalar(out, out, 0.5, None, ALU.mult))
    link(nc.vector.reciprocal(out, out))


def setup_and_stats(nc, sem, x, wqk, wv, dwqk, dwv, g96, gsel, g112, wqk_dense, wv_pair, g112_sb,
                    gn0_scale, gn0_bias, top_scale, top_bias, end_scale, end_bias):
    CH, FM = 8192, 512
    NCH = H * W // CH
    PER = CH // FM
    BC = B * C
    xv = x.rearrange("b c h w -> (b c) (h w)").rearrange("p (n f) -> p n f", f=CH)
    with ExitStack() as ctx:
        def sb(name, shape):
            return ctx.enter_context(nc.sbuf_tensor(name, shape, F32))

        xs = sb("xs", [BC, 2, CH])
        stats = sb("stats", [BC, NCH * PER, 6])
        mv = sb("mv", [BC, 2])
        diff = sb("diff", [BC, 1])
        var = sb("var", [PP, B])
        root = sb("root", [PP, B])
        g96_sb = sb("g96_sb", [BC, BC])
        gsel_sb = sb("gsel_sb", [BC, B, PP])
        wqkT = sb("wqkT", [PP, 2 * C])
        wvT = sb("wvT", [PP, C])
        dqk = sb("dqk", [PP, CFG, 3, 2 * C])
        dv = sb("dv", [PP, CFG, 3, C])
        wv_dense = sb("wv_dense", [PP, CFG, 3, C])
        ps_mean = ctx.enter_context(nc.psum_tensor("ps_mean", [BC, 512], F32))
        ps_sel = ctx.enter_context(nc.psum_tensor("ps_sel", [PP, 512], F32))

        cleared, params = sem("cleared"), sem("params")
        chunk = [sem("chunk0"), sem("chunk1")]
        chunk_used = [sem("chunk_used0"), sem("chunk_used1")]
        dv_step = sem("setup_dve")
        mean_ready, group_mean, mv_ready, group_mv = sem("mean_ready"), sem("group_mean"), sem("mv_ready"), sem("group_mv")
        var_ready, root_ready = sem("var_ready"), sem("root_ready")
        NPARAM = 3 + 2 + 2 + 2 * 6

        with nc.Block() as block:
            @block.sync
            def _(sp):
                sp.dma_start(xs[:, 0], xv[:, 0]).then_inc(chunk[0], 16)
                sp.dma_start(xs[:, 1], xv[:, 1]).then_inc(chunk[1], 16)
                sp.dma_start(g96_sb[:], g96).then_inc(params, 16)
                sp.dma_start(gsel_sb[:], gsel).then_inc(params, 16)
                sp.dma_start(g112_sb[:], g112).then_inc(params, 16)
                sp.wait_ge(cleared, 1)
                for r in range(2):
                    half = slice(ODD * r, ODD * r + C)
                    sp.dma_start(wqkT[half, :], wqk).then_inc(params, 16)
                    sp.dma_start(wvT[half, :], wv).then_inc(params, 16)
                for cfg, r, ty in ((0, 0, 0), (0, 1, 1), (1, 0, 2), (2, 1, 0), (3, 0, 1), (3, 1, 2)):
                    half = slice(ODD * r, ODD * r + C)
                    sp.dma_start(dqk[half, cfg], dwqk[ty].unsqueeze(0).broadcast_to([C, 3, 2 * C])).then_inc(params, 16)
                    sp.dma_start(dv[half, cfg], dwv[ty].unsqueeze(0).broadcast_to([C, 3, C])).then_inc(params, 16)
                with sp.Fori(1, NCH // 2) as i:
                    for s in range(2):
                        sp.wait_ge(chunk_used[s], i)
                        sp.dma_start(xs[:, s], xv[:, bass.ds(2 * i + s, 1)]).then_inc(chunk[s], 16)

            @block.vector
            def _(v):
                for t in (wqkT, wvT, dqk, dv):
                    nc.vector.memset(t[:], 0.0)
                nc.vector.memset(wv_pair[:], 0.0).then_inc(cleared, 1)
                with v.Fori(0, NCH // 2) as i:
                    for s in range(2):
                        v.wait_ge(chunk[s], 16 * i + 16)
                        for j in range(PER):
                            last = nc.vector.bn_stats(stats[:, bass.ds((2 * i + s) * PER + j, 1), :],
                                                      xs[:, s, j * FM:(j + 1) * FM])
                        last.then_inc(chunk_used[s], 1)
                n = [0]

                def link(ins):
                    n[0] += 1
                    ins.then_inc(dv_step, 1)
                    v.wait_ge(dv_step, n[0])

                v.wait_ge(chunk_used[1], NCH // 2)
                link(nc.vector.bn_aggr(mv[:], stats[:]))
                nc.vector.tensor_copy(diff[:], mv[:, 0:1]).then_inc(mean_ready, 1)
                v.wait_ge(group_mean, 1)
                link(nc.vector.tensor_tensor(diff[:], mv[:, 0:1], ps_mean[:, 0:1], ALU.subtract))
                link(nc.vector.tensor_tensor(diff[:], diff[:], diff[:], ALU.mult))
                nc.vector.tensor_tensor(mv[:, 1:2], mv[:, 1:2], diff[:], ALU.add).then_inc(mv_ready, 1)
                v.wait_ge(group_mv, 1)
                sel = ps_sel[:, 0:2 * B].rearrange("p (b two) -> p b two", two=2)
                nc.vector.tensor_scalar(var[:], sel[:, :, 1], GN_EPS, None, ALU.add).then_inc(var_ready, 1)
                v.wait_ge(root_ready, 1)
                inverse_root(nc, link, gn0_scale[:], var[:], root[:])
                link(nc.vector.scalar_tensor_tensor(gn0_bias[:], sel[:, :, 0], -1.0, gn0_scale[:], ALU.mult, ALU.mult))
                for src, top, end in ((gn0_scale, top_scale, end_scale), (gn0_bias, top_bias, end_bias)):
                    for tab in (top, end):
                        link(nc.vector.tensor_copy(tab[:], src[:].unsqueeze(2).broadcast_to([PP, B, G])))
                    nc.vector.memset(top[0:C, :, 0], 0.0)
                    link(nc.vector.memset(end[ODD:PP, :, G - 1], 0.0))
                v.wait_ge(params, 16 * NPARAM)
                for cfg in range(CFG):
                    for tx in range(3):
                        nc.vector.tensor_tensor(wqk_dense[:, cfg, tx], dqk[:, cfg, tx], wqkT[:], ALU.mult)
                        link(nc.vector.tensor_tensor(wv_dense[:, cfg, tx], dv[:, cfg, tx], wvT[:], ALU.mult))
                for pair in range(2):
                    for row in range(2):
                        link(nc.vector.tensor_copy(wv_pair[:, pair, :, ODD * row:ODD * row + C],
                                                   wv_dense[:, pair + 2 * row]))

            @block.scalar
            def _(act):
                act.wait_ge(var_ready, 1)
                nc.scalar.activation(root[:], var[:], ACT.Sqrt).then_inc(root_ready, 1)

            @block.tensor
            def _(pe):
                pe.wait_ge(params, 16 * NPARAM)
                pe.wait_ge(mean_ready, 1)
                nc.tensor.matmul(ps_mean[:, 0:1], g96_sb[:], diff[:], start=True, stop=True).then_inc(group_mean, 1)
                pe.wait_ge(mv_ready, 1)
                for b in range(B):
                    last = nc.tensor.matmul(ps_sel[:, 2 * b:2 * b + 2], gsel_sb[:, b], mv[:], start=True, stop=True)
                last.then_inc(group_mv, 1)


def load_pairs(eng, x, b, dst, g, landed, top=False, end=False):
    rows = x[b].rearrange("c (m two) w -> two c m w", two=2)
    a = 1 if top else 0
    e = NQ - 1 if end else NQ
    if top or end:
        eng.dma_start(dst[0:C, a:NQ], rows[1, :, NP * g - 1 + a:NP * g - 1 + NQ]).then_inc(landed, 16)
        eng.dma_start(dst[ODD:PP, 0:e], rows[0, :, NP * g:NP * g + e]).then_inc(landed, 16)
    else:
        eng.dma_start(dst[0:C, :], rows[1, :, bass.ds(NP * g - 1, NQ)]).then_inc(landed, 16)
        eng.dma_start(dst[ODD:PP, :], rows[0, :, bass.ds(NP * g, NQ)]).then_inc(landed, 16)


def normalised(nc, norm0, b, g, q, out, in_):
    gn0_scale, gn0_bias, top_scale, top_bias, end_scale, end_bias = norm0
    if q == 0:
        scale, bias = top_scale[:, b, bass.ds(g, 1)], top_bias[:, b, bass.ds(g, 1)]
    elif q == NQ - 1:
        scale, bias = end_scale[:, b, bass.ds(g, 1)], end_bias[:, b, bass.ds(g, 1)]
    else:
        scale, bias = gn0_scale[:, b:b + 1], gn0_bias[:, b:b + 1]
    return nc.scalar.activation(out, in_, ACT.Identity, bias=bias, scale=scale)


def attention(nc, sem, x, wqk_dense, norm0, projT, temp, ident, mixers):
    HQ = 2 * HEADS
    with ExitStack() as ctx:
        def sb(name, shape):
            return ctx.enter_context(nc.sbuf_tensor(name, shape, F32))

        def psum(name, shape):
            return ctx.enter_context(nc.psum_tensor(name, shape, F32))

        sumsq = sb("sumsq", [TOK, B, HQ, HD])
        ones = sb("ones", [TOK, HD])
        gram = [psum(f"gram{b}", [HD, 2, 512]) for b in range(B)]

        def gram_of(b, h):
            return gram[b][:, h // 4, (h % 4) * HD:(h % 4 + 1) * HD]

        with ExitStack() as inner:
            def sbi(name, shape):
                return inner.enter_context(nc.sbuf_tensor(name, shape, F32))

            raw = sbi("raw", [PP, 2, NQ, W])
            xd = sbi("xd", [PP, 2, NQ, N, TOK + 2])
            qk = sbi("qk", [TOK, 2, HQ, N * N, HC])
            sq = sbi("sq", [TOK, HQ * HD])
            zero_row = sbi("zero_row", [TOK, 512])
            conv_ps = inner.enter_context(nc.psum_tensor("conv_ps", [TOK, 2, 512], F32))
            ready0 = sem("qk_ready0")
            ready1 = sem("qk_ready1")
            raw_in = [[sem(f"qk_raw_in{b}{s}") for s in range(2)] for b in range(B)]
            norm_done = [sem(f"qk_norm_done{b}") for b in range(B)]
            conv_done = [sem(f"qk_conv_done{b}") for b in range(B)]
            act_moved = [sem(f"qk_act_moved{b}") for b in range(B)]
            dve_moved = [sem(f"qk_dve_moved{b}") for b in range(B)]
            gram_done = [sem(f"gram_done{b}") for b in range(B)]
            squared = [sem(f"squared{b}") for b in range(B)]
            sq_ready = [sem(f"sq_ready{b}") for b in range(B)]
            sums_clear = sem("sums_clear")

            def move(engine, b, slot, dy):
                src = conv_ps[:, dy % 2, 0:N * 2 * C].rearrange("p (d h c) -> p h d c", d=N, c=HC)
                return engine(qk[:, slot, :, N * dy:N * dy + N, :], src)

            with nc.Block() as block:
                @block.gpsimd
                def _(pool):
                    nc.gpsimd.memset(raw[:], 0.0)
                    nc.gpsimd.memset(xd[:], 0.0).then_inc(ready0, 1)

                @block.sync
                def _(sp):
                    sp.wait_ge(ready0, 1)
                    for b in range(B):
                        for s in range(2):
                            if b:
                                sp.wait_ge(norm_done[b - 1], G - 1 + s)
                            load_pairs(sp, x, b, raw[:, s], s, raw_in[b][s], top=s == 0)
                        with sp.Fori(1, G // 2 - 1) as i:
                            for s in range(2):
                                sp.wait_ge(norm_done[b], 2 * i + s - 1)
                                load_pairs(sp, x, b, raw[:, s], 2 * i + s, raw_in[b][s])
                        for s in range(2):
                            sp.wait_ge(norm_done[b], G - 3 + s)
                            load_pairs(sp, x, b, raw[:, s], G - 2 + s, raw_in[b][s], top=s == 0 and G == 2, end=s == 1)

                @block.scalar
                def _(act):
                    def norm(b, g, s, q, n_in):
                        if q == 0:
                            act.wait_ge(raw_in[b][s], n_in)
                        ins = normalised(nc, norm0, b, g, q,
                                         xd[:, s, q, :, 1:TOK + 1],
                                         raw[:, s, q].rearrange("p (j m) -> p m j", m=N))
                        if q == NQ - 1:
                            ins.then_inc(norm_done[b], 1)

                    def group(b, g, s, first, last_group=False):
                        q = 0
                        for i in range(NB):
                            for dy in (0, 2):
                                n = NB * g + i
                                if not last_group:
                                    if q == 0 and not first:
                                        act.wait_ge(conv_done[b], N * NB * g)
                                    for _ in range(2 if i == NB - 1 and dy == 2 else 1):
                                        norm(b, g + 1, 1 - s, q, 32 * ((g + 1 - (1 - s)) // 2) + 32
                                             if isinstance(g, int) else (16 * (g + 1 - (1 - s)) + 32))
                                        q += 1
                                if not (first and i < 2):
                                    act.wait_ge(gram_done[b], n - 1)
                                    act.wait_ge(squared[b], n - 1)
                                act.wait_ge(conv_done[b], N * n + dy + 1)
                                move(nc.scalar.copy, b, i % 2, dy).then_inc(act_moved[b], 1)

                    act.wait_ge(ready0, 1)
                    for b in range(B):
                        if b:
                            act.wait_ge(conv_done[b - 1], N * NB * G)
                            act.wait_ge(gram_done[b - 1], NB * G)
                            act.wait_ge(squared[b - 1], NB * G)
                        for q in range(NQ):
                            norm(b, 0, 0, q, 32)
                        group(b, 0, 0, True)
                        group(b, 1, 1, False)
                        with act.Fori(1, G // 2 - 1) as i:
                            group(b, 2 * i, 0, False)
                            group(b, 2 * i + 1, 1, False)
                        group(b, G - 2, 0, False)
                        group(b, G - 1, 1, False, last_group=True)

                @block.tensor
                def _(pe):
                    def gram_block(b, n, slot):
                        pe.wait_ge(act_moved[b], 2 * n + 2)
                        pe.wait_ge(dve_moved[b], 2 * n + 2)
                        for h in range(HEADS):
                            last = nc.tensor.matmul(gram_of(b, h), flat(qk[:, slot, 2 * h]), flat(qk[:, slot, 2 * h + 1]),
                                                    start=False, stop=False, skip_group_check=True)
                        last.then_inc(gram_done[b], 1)

                    def group(b, g, s, first):
                        pe.wait_ge(norm_done[b], g + 1)
                        for i in range(NB):
                            n = NB * g + i
                            for dy in range(N):
                                if not (first and i == 0 and dy < 2):
                                    if dy % 2 == 0:
                                        pe.wait_ge(act_moved[b], 2 * n + dy // 2)
                                    else:
                                        pe.wait_ge(dve_moved[b], 2 * n + dy // 2)
                                k = 0
                                for col in (0, 1, 2, 3, -1, N):
                                    lo, hi = max(0, col - 1), min(N - 1, col + 1)
                                    start = col // N + 1
                                    for pair in range(2):
                                        last = nc.tensor.matmul(
                                            conv_ps[:, dy % 2, lo * 2 * C:(hi + 1) * 2 * C],
                                            xd[:, s, 2 * i + dy // 2 + pair, col % N, start:start + TOK],
                                            flat(wqk_dense[:, pair + 2 * (dy % 2), lo - col + 1:hi - col + 2]),
                                            start=k == 0, stop=k == 11, skip_group_check=True)
                                        k += 1
                                last.then_inc(conv_done[b], 1)
                                if dy == 0 and not (first and i == 0):
                                    gram_block(b, n - 1, (i - 1) % 2)

                    pe.wait_ge(ready1, 1)
                    for b in range(B):
                        for half in range(2):
                            nc.tensor.matmul(gram[b][:, half], zero_row[:, 0:HD], zero_row[:], start=True, stop=False,
                                             skip_group_check=True)
                        if b:
                            pe.wait_ge(act_moved[b - 1], 2 * NB * G)
                            pe.wait_ge(dve_moved[b - 1], 2 * NB * G)
                        group(b, 0, 0, True)
                        group(b, 1, 1, False)
                        with pe.Fori(1, G // 2) as i:
                            group(b, 2 * i, 0, False)
                            group(b, 2 * i + 1, 1, False)
                        gram_block(b, NB * G - 1, (NB - 1) % 2)

                @block.vector
                def _(v):
                    nc.vector.memset(zero_row[:], 0.0).then_inc(ready1, 1)
                    nc.vector.memset(ones[:], 1.0)
                    nc.vector.memset(sumsq[:], 0.0).then_inc(sums_clear, 1)
                    v.wait_ge(sums_clear, 1)

                    def group(b, g, first):
                        for i in range(NB):
                            n = NB * g + i
                            if not (first and i < 2):
                                v.wait_ge(gram_done[b], n - 1)
                            for dy in (1, 3):
                                v.wait_ge(conv_done[b], N * n + dy + 1)
                                move(nc.vector.tensor_copy, b, i % 2, dy).then_inc(dve_moved[b], 1)
                            v.wait_ge(act_moved[b], 2 * n + 2)
                            v.wait_ge(dve_moved[b], 2 * n + 2)
                            all_qk = qk[:, i % 2].rearrange("p h s c -> p (h s c)")
                            nc.vector.tensor_tensor(sq[:], all_qk, all_qk, ALU.mult).then_inc(sq_ready[b], 1)
                            v.wait_ge(sq_ready[b], n + 1)
                            if not (first and i == 0):
                                v.wait_ge(squared[b], n)
                            sums = sumsq[:, b].rearrange("p h d -> p (h d)")
                            nc.vector.tensor_tensor(sums, sums, sq[:], ALU.add).then_inc(squared[b], 1)

                    for b in range(B):
                        group(b, 0, True)
                        group(b, 1, False)
                        with v.Fori(1, G // 2) as i:
                            group(b, 2 * i, False)
                            group(b, 2 * i + 1, False)

        softmax_and_mixers(nc, sem, sumsq, ones, gram_of, projT, temp, ident, mixers)


def softmax_and_mixers(nc, sem, sumsq, ones, gram_of, projT, temp, ident, mixers):
    HQ = 2 * HEADS
    PC = N * N * C
    with ExitStack() as ctx:
        def sb(name, shape):
            return ctx.enter_context(nc.sbuf_tensor(name, shape, F32))

        proj = sb("proj", [HD, HEADS, PC])
        temp_sb = sb("temp_sb", [HD, HEADS])
        eye = sb("eye", [HD, HD])
        rnorm = sb("rnorm", [HD, B, HQ])
        norm2 = sb("norm2", [HD, HQ])
        norm = sb("norm", [HD, HQ])
        diag = sb("diag", [HD, HEADS, HD])
        att = sb("att", [HD, HEADS, HD])
        prob = sb("prob", [HD, HEADS, HD])
        top = sb("top", [HD, HEADS])
        total = sb("total", [HD, HEADS])
        mix = sb("mix", [HD, HEADS, PC])
        ps = ctx.enter_context(nc.psum_tensor("att_ps", [HD, 2, 512], F32))
        cleared, params, norms, scaled = sem("proj_cleared"), sem("att_params"), sem("norms"), sem("diag_ready")
        spread, negmax, exped, probs = sem("spread"), sem("negmax"), sem("exped"), sem("probs")
        mixed, mix_moved, stored, step = sem("mixed"), sem("mix_moved"), sem("mix_stored"), sem("att_step")
        norm2_ready, norm_ready = sem("norm2_ready"), sem("norm_ready")
        NPARAM = 2 + N * N

        with nc.Block() as block:
            @block.sync
            def _(sp):
                sp.dma_start(temp_sb[:], temp.broadcast_to([HD, HEADS])).then_inc(params, 16)
                sp.dma_start(eye[:], ident).then_inc(params, 16)
                sp.wait_ge(cleared, 1)
                for p in range(N * N):
                    sp.dma_start(proj[HC * p:HC * p + HC, :, C * p:C * p + C],
                                 projT.rearrange("(h c) o -> c h o", c=HC)).then_inc(params, 16)
                for b in range(B):
                    sp.wait_ge(mix_moved, 2 * HEADS * (b + 1))
                    for e in range(N * N):
                        sp.dma_start(mixers[b, e].rearrange("h c n -> c h n"),
                                     mix[HC * e:HC * e + HC]).then_inc(stored, 16)
                    sp.wait_ge(stored, 16 * N * N * (b + 1))

            @block.vector
            def _(v):
                n = [0]

                def link(ins):
                    n[0] += 1
                    ins.then_inc(step, 1)
                    v.wait_ge(step, n[0])

                nc.vector.memset(proj[:], 0.0).then_inc(cleared, 1)
                v.wait_ge(params, 16 * NPARAM)
                for b in range(B):
                    v.wait_ge(norms, b + 1)
                    nc.vector.tensor_scalar(norm2[:], ps[:, 0, 0:HQ], 1e-24, None, ALU.max).then_inc(norm2_ready, 1)
                    v.wait_ge(norm_ready, b + 1)
                    inverse_root(nc, link, rnorm[:, b], norm2[:], norm[:])
                    rk = rnorm[:, b].rearrange("p (h two) -> p h two", two=2)[:, :, 1]
                    link(nc.vector.tensor_tensor(rk, rk, temp_sb[:], ALU.mult))
                    for h in range(HEADS):
                        ins = nc.vector.tensor_scalar(diag[:, h], eye[:], rnorm[:, b, 2 * h + 1:2 * h + 2], None, ALU.mult)
                    ins.then_inc(scaled, 1)
                    v.wait_ge(spread, b + 1)
                    for h in range(HEADS):
                        fac = ps[:, h // 4, (h % 4) * HD:(h % 4 + 1) * HD]
                        nc.vector.tensor_copy(diag[:, h], fac)
                        link(nc.vector.tensor_scalar(att[:, h], gram_of(b, h), rnorm[:, b, 2 * h:2 * h + 1], None, ALU.mult))
                    link(nc.vector.tensor_tensor(att[:], att[:], diag[:], ALU.mult))
                    link(nc.vector.tensor_reduce(top[:], att[:], AX.X, ALU.max))
                    nc.vector.tensor_scalar(top[:], top[:], -1.0, None, ALU.mult).then_inc(negmax, 1)
                    v.wait_ge(exped, HEADS * (b + 1))
                    link(nc.vector.reciprocal(total[:], total[:]))
                    for h in range(HEADS):
                        ins = nc.vector.tensor_scalar(prob[:, h], prob[:, h], total[:, h:h + 1], None, ALU.mult)
                    ins.then_inc(probs, 1)
                    for k in range(2 * HEADS):
                        h, half = k // 2, k % 2
                        if b and k == 0:
                            v.wait_ge(stored, 16 * N * N * b)
                        v.wait_ge(mixed, 2 * HEADS * b + k + 1)
                        nc.vector.tensor_copy(mix[:, h, half * PC // 2:(half + 1) * PC // 2],
                                              ps[:, half, 0:PC // 2]).then_inc(mix_moved, 1)

            @block.scalar
            def _(act):
                for b in range(B):
                    act.wait_ge(norm2_ready, b + 1)
                    nc.scalar.activation(norm[:], norm2[:], ACT.Sqrt).then_inc(norm_ready, 1)
                    act.wait_ge(negmax, b + 1)
                    for h in range(HEADS):
                        nc.scalar.activation(prob[:, h], att[:, h], ACT.Exp, bias=top[:, h:h + 1],
                                             accum_out=total[:, h:h + 1]).then_inc(exped, 1)

            @block.tensor
            def _(pe):
                pe.wait_ge(params, 16 * NPARAM)
                for b in range(B):
                    if b:
                        pe.wait_ge(mix_moved, 2 * HEADS * b)
                    for k in range(HQ):
                        last = nc.tensor.matmul(ps[:, 0, k:k + 1], sumsq[:, b, k], ones[:, 0:1], start=True, stop=True)
                    last.then_inc(norms, 1)
                    pe.wait_ge(scaled, b + 1)
                    for half in range(2):
                        last = nc.tensor.matmul(ps[:, half, 0:4 * HD], ones[0:HD, :],
                                                flat(diag[:, 4 * half:4 * half + 4]), start=True, stop=True)
                    last.then_inc(spread, 1)
                    pe.wait_ge(probs, b + 1)
                    for k in range(2 * HEADS):
                        h, half = k // 2, k % 2
                        if k >= 2:
                            pe.wait_ge(mix_moved, 2 * HEADS * b + k - 1)
                        nc.tensor.matmul(ps[:, half, 0:PC // 2], prob[:, h], proj[:, h, half * PC // 2:(half + 1) * PC // 2],
                                         start=True, stop=True).then_inc(mixed, 1)


def mix_values(nc, sem, b, x, wv_pair, norm0, mixers, x1_scan, x1_rows, x1_stats):
    NK = 2 * N
    NM = N * N // 2
    NBANK = 4
    with ExitStack() as ctx:
        def sb(name, shape):
            return ctx.enter_context(nc.sbuf_tensor(f"{name}_b{b}", shape, F32))

        def s_(name):
            return sem(f"{name}_b{b}")

        raw = sb("mv_raw", [PP, 2, NQ, W])
        xn = sb("mv_xn", [PP, NQ, W + 2])
        v_sb = sb("v_sb", [PP, NP, N, TOK])
        mixT = sb("mixT", [PP, NK, NM, PP])
        scan_t = sb("scan_t", [PP, 2, T, W2])
        rows_t = sb("rows_t", [PP, 2, NP, W])
        v_ps = ctx.enter_context(nc.psum_tensor(f"v_ps{b}", [PP, 2, 512], F32))
        o_ps = ctx.enter_context(nc.psum_tensor(f"o_ps{b}", [PP, NBANK, 512], F32))
        cleared, raw_clear, mix_in = s_("mix_cleared"), s_("raw_clear"), s_("mix_in")
        raw_in = [s_("mv_raw_in0"), s_("mv_raw_in1")]
        norm_done, v_done, v_moved, o_done = s_("mv_norm_done"), s_("v_done"), s_("v_moved"), s_("o_done")
        summed, rows_done, stats_done = s_("summed"), s_("rows_done"), s_("x1_stats_done")
        scan_out = [s_("scan_out0"), s_("scan_out1")]
        rows_out = [s_("rows_out0"), s_("rows_out1")]

        with nc.Block() as block:
            @block.gpsimd
            def _(pool):
                nc.gpsimd.memset(raw[:], 0.0)
                nc.gpsimd.memset(xn[:], 0.0).then_inc(raw_clear, 1)

            @block.sync
            def _(sp):
                sp.wait_ge(raw_clear, 1)
                load_pairs(sp, x, b, raw[:, 0], 0, raw_in[0], top=True)
                sp.wait_ge(cleared, 1)
                for r in range(2):
                    for e2 in range(2):
                        for ex in range(N):
                            src = mixers[b, (2 * e2 + r) * N + ex].rearrange("h c (m q o) -> q (h c) m o", m=NM, q=2)
                            for q in range(2):
                                sp.dma_start(mixT[ODD * r:ODD * r + C, e2 * N + ex, :, ODD * q:ODD * q + C],
                                             src[q]).then_inc(mix_in, 16)
                load_pairs(sp, x, b, raw[:, 1], 1, raw_in[1])

                def store(g, s):
                    sp.wait_ge(summed, NM * g + NM)
                    sp.dma_start(x1_scan[bass.ds(g, 1), :, :, b].rearrange("g p t w -> (g p) t w"), scan_t[:, s]).then_inc(scan_out[s], 16)
                    sp.wait_ge(rows_done, N * g + N)
                    sp.dma_start(x1_rows[b, bass.ds(g, 1)].rearrange("g p t w -> (g p) t w"), rows_t[:, s]).then_inc(rows_out[s], 16)

                with sp.Fori(1, G // 2 - 1) as i:
                    for s in range(2):
                        store(2 * i + s - 2, s)
                        load_pairs(sp, x, b, raw[:, s], 2 * i + s, raw_in[s])
                for s in range(2):
                    store(G - 4 + s, s)
                    load_pairs(sp, x, b, raw[:, s], G - 2 + s, raw_in[s], end=s == 1)
                for s in range(2):
                    store(G - 2 + s, s)
                for s in range(2):
                    sp.wait_ge(scan_out[s], 16 * (G // 2))
                    sp.wait_ge(rows_out[s], 16 * (G // 2))

            @block.scalar
            def _(act):
                def norm(g, s, n_in):
                    act.wait_ge(raw_in[s], n_in)
                    for q in range(NQ):
                        ins = normalised(nc, norm0, b, g, q, xn[:, q, 1:W + 1], raw[:, s, q])
                    ins.then_inc(norm_done, 1)

                def group(g, s, first, last=False):
                    for q in range(NP):
                        act.wait_ge(v_done, NP * g + q + 1)
                        if q == 0 and not (first and s == 0):
                            act.wait_ge(o_done, NM * g)
                        nc.scalar.copy(v_sb[:, q], v_ps[:, q % 2].rearrange("p (j m) -> p m j", m=N)).then_inc(v_moved, 1)
                    if not last:
                        norm(g + 1, 1 - s, 16 * (g + 1 - (1 - s)) + 32)
                    if not first:
                        act.wait_ge(rows_out[s], 8 * (g - s))
                    for dy in range(N):
                        act.wait_ge(summed, NM * g + 2 * dy + 2)
                        for q in range(2):
                            ins = nc.scalar.copy(
                                rows_t[ODD * (dy % 2):ODD * (dy % 2) + C, s, dy // 2:NP:2, q:W:2],
                                scan_t[ODD * q:ODD * q + C, s, dy:T:N, :])
                        ins.then_inc(rows_done, 1)

                act.wait_ge(raw_clear, 1)
                act.wait_ge(cleared, 1)
                norm(0, 0, 32)
                group(0, 0, True)
                group(1, 1, True)
                with act.Fori(1, G // 2 - 1) as i:
                    group(2 * i, 0, False)
                    group(2 * i + 1, 1, False)
                group(G - 2, 0, False)
                group(G - 1, 1, False, last=True)

            @block.tensor
            def _(pe):
                def group(g, s, first):
                    pe.wait_ge(norm_done, g + 1)
                    for q in range(NP):
                        if not (first and s == 0 and q < 2):
                            pe.wait_ge(v_moved, NP * g + q - 1)
                        for k in range(6):
                            pair, tx = k // 3, k % 3
                            last = nc.tensor.matmul(v_ps[:, q % 2], wv_pair[:, pair, tx], xn[:, q + pair, 2 - tx:2 - tx + W],
                                                    start=k == 0, stop=k == 5)
                        last.then_inc(v_done, 1)
                    pe.wait_ge(v_moved, NP * g + NP)
                    for m in range(NM):
                        if not (first and s == 0 and m < NBANK):
                            pe.wait_ge(summed, NM * g + m - NBANK + 1)
                        for k in range(NK):
                            last = nc.tensor.matmul(o_ps[:, m % NBANK], mixT[:, k, m], v_sb[:, k // N:NP:2, k % N, :],
                                                    start=k == 0, stop=k == NK - 1)
                        last.then_inc(o_done, 1)

                pe.wait_ge(mix_in, 16 * 2 * 2 * NK)
                group(0, 0, True)
                group(1, 1, False)
                with pe.Fori(1, G // 2) as i:
                    group(2 * i, 0, False)
                    group(2 * i + 1, 1, False)

            @block.vector
            def _(v):
                nc.vector.memset(scan_t[:], 0.0)
                nc.vector.memset(rows_t[:], 0.0)
                nc.vector.memset(mixT[:], 0.0).then_inc(cleared, 1)
                v.wait_ge(cleared, 1)

                def group(g, s, first):
                    if not first:
                        v.wait_ge(scan_out[s], 8 * (g - s))
                        v.wait_ge(rows_done, N * (g - 1))
                    for m in range(NM):
                        dy, dx2 = m // 2, m % 2
                        r, q0 = (dy + 1) % 2, (dy + 1) // 2
                        v.wait_ge(o_done, NM * g + m + 1)
                        for q in range(2):
                            ins = nc.vector.tensor_tensor(
                                scan_t[ODD * q:ODD * q + C, s, dy:T:N, dx2:W2:2],
                                o_ps[ODD * q:ODD * q + C, m % NBANK].rearrange("p (i j) -> p i j", j=TOK),
                                raw[ODD * r:ODD * r + C, s, q0:q0 + 2 * NB - 1:2, 2 * dx2 + q:W:N], ALU.add)
                        ins.then_inc(summed, 1)
                        if dx2:
                            v.wait_ge(summed, NM * g + m + 1)
                            for half in range(2):
                                at = dy + 2 * N * half
                                ins = nc.vector.bn_stats(x1_stats[:, b, bass.ds(NP * g + 2 * dy + half, 1), :],
                                                         scan_t[:, s, at:at + N + 1:N, :])
                    ins.then_inc(stats_done, 1)

                for g in range(2):
                    group(g, g, True)
                with v.Fori(1, G // 2) as i:
                    group(2 * i, 0, False)
                    group(2 * i + 1, 1, False)


def combine_stats(nc, sem, x1_stats, g112_sb, gn1_scale, gn1_bias):
    with ExitStack() as ctx:
        mean = ctx.enter_context(nc.sbuf_tensor("gn1_mean", [PP, B], F32))
        var = ctx.enter_context(nc.sbuf_tensor("gn1_var", [PP, B], F32))
        mv = ctx.enter_context(nc.sbuf_tensor("gn1_mv", [PP, B, 2], F32))
        off = ctx.enter_context(nc.sbuf_tensor("gn1_off", [PP, B], F32))
        gm = ctx.enter_context(nc.sbuf_tensor("gn1_gm", [PP, B], F32))
        root = ctx.enter_context(nc.sbuf_tensor("gn1_root", [PP, B], F32))
        sum_ready, root_ready = sem("gn1_sum_ready"), sem("gn1_root_ready")
        ps = ctx.enter_context(nc.psum_tensor("gn1_ps", [PP, 2, 512], F32))
        step, mean_ready, group_mean, var_ready, group_var = (
            sem("gn1_step"), sem("gn1_mean_ready"), sem("gn1_group_mean"), sem("gn1_var_ready"), sem("gn1_group_var"))
        with nc.Block() as block:
            @block.vector
            def _(v):
                n = [0]

                def link(ins):
                    n[0] += 1
                    ins.then_inc(step, 1)
                    v.wait_ge(step, n[0])

                for b in range(B):
                    link(nc.vector.bn_aggr(mv[:, b], x1_stats[:, b]))
                nc.vector.tensor_copy(mean[:], mv[:, :, 0]).then_inc(mean_ready, 1)
                v.wait_ge(group_mean, 1)
                link(nc.vector.tensor_copy(gm[:], ps[:, 0, 0:B]))
                link(nc.vector.tensor_tensor(off[:], mean[:], gm[:], ALU.subtract))
                link(nc.vector.tensor_tensor(off[:], off[:], off[:], ALU.mult))
                nc.vector.tensor_tensor(var[:], mv[:, :, 1], off[:], ALU.add).then_inc(var_ready, 1)
                v.wait_ge(group_var, 1)
                nc.vector.tensor_scalar(var[:], ps[:, 1, 0:B], GN_EPS, None, ALU.add).then_inc(sum_ready, 1)
                v.wait_ge(root_ready, 1)
                inverse_root(nc, link, gn1_scale[:], var[:], root[:])
                link(nc.vector.scalar_tensor_tensor(gn1_bias[:], gm[:], -1.0, gn1_scale[:], ALU.mult, ALU.mult))

            @block.scalar
            def _(act):
                act.wait_ge(sum_ready, 1)
                nc.scalar.activation(root[:], var[:], ACT.Sqrt).then_inc(root_ready, 1)

            @block.tensor
            def _(pe):
                pe.wait_ge(mean_ready, 1)
                nc.tensor.matmul(ps[:, 0, 0:B], g112_sb[:], mean[:], start=True, stop=True).then_inc(group_mean, 1)
                pe.wait_ge(var_ready, 1)
                nc.tensor.matmul(ps[:, 1, 0:B], g112_sb[:], var[:], start=True, stop=True).then_inc(group_var, 1)


def scan(nc, sem, way, taps, bias, src, dst, scale1, bias1):
    LP = W2
    n_params = 2 * K + 2 + (way == "up")
    with ExitStack() as ctx:
        def sb(name, shape):
            return ctx.enter_context(nc.sbuf_tensor(f"{way}_{name}", shape, F32))

        def s_(name):
            return sem(f"{way}_{name}")

        u_in = sb("u_in", [PP, 2, T * B * LP])
        o_t = sb("o_t", [PP, 2, T * B * LP])
        state = sb("state", [PP, B, 2, LP + 2])
        w_sb = sb("taps", [PP, 3, PP])
        b_sb = sb("bias", [PP, 1])
        ps = ctx.enter_context(nc.psum_tensor(f"{way}_ps", [PP, B, 512], F32))
        cleared, params = s_("cleared"), s_("params")
        loaded = [s_("loaded0"), s_("loaded1")]
        stored = [s_("stored0"), s_("stored1")]
        conv_done = [s_("conv_done0"), s_("conv_done1")]
        state_done = [s_("state_done0"), s_("state_done1")]
        copied = [s_("copied0"), s_("copied1")]
        normed = s_("normed")
        norm = scale1 is not None
        LOADS = 2 if way == "up" else 1
        STORES = 2 if way == "up" else 1

        def line(s, k, b):
            if way == "right":
                return u_in[:, s].rearrange("p (b n t) -> p b n t", b=B, t=T)[:, b, :, k]
            at = k if way == "down" else T - 1 - k
            return u_in[:, s].rearrange("p (t b n) -> p t b n", b=B, t=T)[:, at, b]

        with nc.Block() as block:
            @block.sync
            def _(sp):
                sp.wait_ge(cleared, 1)
                for r in range(2):
                    sp.dma_start(b_sb[ODD * r:ODD * r + C], bias).then_inc(params, 16)
                    for shift in range(3):
                        for q in range(2):
                            k = 2 * (shift - 1) + r - q + K // 2
                            if 0 <= k < K:
                                sp.dma_start(w_sb[ODD * r:ODD * r + C, shift, ODD * q:ODD * q + C],
                                             taps[k]).then_inc(params, 16)

                def one(t, g):
                    return t[bass.ds(g, 1)]

                def load(g, s, first=False, last=False):
                    if way != "up":
                        at = g * -1 + (G - 1) if way == "left" else g
                        tile = one(src, at).rearrange("g p a b c -> (g p) (a b c)")
                        sp.dma_start(u_in[:, s], tile).then_inc(loaded[s], 16)
                        return
                    rows = u_in[:, s].rearrange("p (t x) -> p t x", t=T)
                    here = one(src, g * -1 + (G - 1)).rearrange("g p t b n -> (g p) t (b n)")
                    before = one(src, G - 1 if last else g * -1 + (G - 2)).rearrange("g p t b n -> (g p) t (b n)")
                    if first:
                        sp.dma_start(rows[:, T - 1:T], here[:, T - 1:T]).then_inc(params, 16)
                        sp.dma_start(rows[:, 1:T - 1], here[:, 0:T - 2]).then_inc(loaded[s], 16)
                    else:
                        sp.dma_start(rows[:, 1:T], here[:, 0:T - 1]).then_inc(loaded[s], 16)
                    sp.dma_start(rows[:, 0:1], before[:, T - 1:T]).then_inc(loaded[s], 16)

                def store(g, s):
                    for b in range(B):
                        sp.wait_ge(copied[b], T * g + T)
                    if way == "up":
                        for b in range(B):
                            tile = o_t[:, s].rearrange("p (b c x) -> p b c x", b=B, c=G)[:, b]
                            sp.dma_start(dst[:, :, b, bass.ds(g * -NP + NP * (G - 1), NP)].rearrange("c p h t -> p c (h t)"),
                                         tile).then_inc(stored[s], 16)
                    else:
                        at = g * -1 + (G - 1) if way == "left" else g
                        sp.dma_start(one(dst, at).rearrange("g p a b c -> (g p) (a b c)"), o_t[:, s]).then_inc(stored[s], 16)

                load(0, 0, first=True)
                load(1, 1)
                with sp.Fori(1, G // 2 - 1) as i:
                    for s in range(2):
                        store(2 * i + s - 2, s)
                        load(2 * i + s, s)
                for s in range(2):
                    store(G - 4 + s, s)
                    load(G - 2 + s, s, last=s == 1)
                for s in range(2):
                    store(G - 2 + s, s)
                for s in range(2):
                    sp.wait_ge(stored[s], 16 * STORES * (G // 2))

            @block.tensor
            def _(pe):
                def steps(g, start):
                    for k in range(start, 2 * T):
                        for b in range(B):
                            pe.wait_ge(state_done[b], T * g + k)
                            for shift in range(3):
                                last = nc.tensor.matmul(ps[:, b, 0:LP], w_sb[:, shift],
                                                        state[:, b, (k - 1) % 2, shift:shift + LP],
                                                        start=shift == 0, stop=shift == 2)
                            last.then_inc(conv_done[b], 1)

                pe.wait_ge(params, 16 * n_params)
                steps(0, 1)
                with pe.Fori(1, G // 2) as i:
                    steps(2 * i, 0)

            @block.vector
            def _(v):
                nc.vector.memset(w_sb[:], 0.0)
                nc.vector.memset(b_sb[:], 0.0)
                nc.vector.memset(state[:], 0.0)
                nc.vector.memset(o_t[32:64], 0.0).then_inc(cleared, 1)
                v.wait_ge(params, 16 * n_params)

                def arrived(g, s):
                    if norm:
                        v.wait_ge(normed, g + 1)
                    else:
                        v.wait_ge(loaded[s], 8 * LOADS * (g - s) + 16 * LOADS)

                arrived(0, 0)
                for b in range(B):
                    nc.vector.tensor_copy(state[:, b, 0, 1:LP + 1], line(0, 0, b)).then_inc(state_done[b], 1)

                def steps(g, start):
                    for k in range(start, 2 * T):
                        if k % T == 0:
                            arrived(g + k // T, k // T)
                        for b in range(B):
                            v.wait_ge(conv_done[b], T * g + k)
                            if start == 0 or k >= 2:
                                v.wait_ge(copied[b], T * g + k - 1)
                            nc.vector.scalar_tensor_tensor(state[:, b, k % 2, 1:LP + 1], ps[:, b, 0:LP], b_sb[:, 0:1],
                                                           line(k // T, k % T, b), ALU.add, ALU.add).then_inc(state_done[b], 1)

                steps(0, 1)
                with v.Fori(1, G // 2) as i:
                    steps(2 * i, 0)

            @block.scalar
            def _(act):
                def norm_line(g, s, k):
                    if k == 0:
                        act.wait_ge(loaded[s], 8 * (g - s) + 16)
                    for b in range(B):
                        ins = nc.scalar.activation(line(s, k, b), line(s, k, b), ACT.Identity,
                                                   bias=bias1[:, b:b + 1], scale=scale1[:, b:b + 1])
                    if k == T - 1:
                        ins.then_inc(normed, 1)

                def copy(s, k, b, ph):
                    st = state[:, b, ph, 1:LP + 1]
                    if way in ("down", "right"):
                        return nc.scalar.copy(o_t[:, s].rearrange("p (t b n) -> p t b n", b=B, t=T)[:, k, b], st)
                    if way == "left":
                        return nc.scalar.copy(o_t[:, s].rearrange("p (b n t) -> p b n t", b=B, t=T)[:, b, :, T - 1 - k], st)
                    r, h = (T - 1 - k) % 2, (T - 1 - k) // 2
                    tile = o_t[:, s].rearrange("p (b c h m q) -> p b c h m q", b=B, c=G, h=NP, q=2)
                    for q in range(2):
                        ins = nc.scalar.copy(tile[ODD * r:ODD * r + C, b, :, h, :, q],
                                             st[ODD * q:ODD * q + C].rearrange("p (c m) -> p c m", c=G))
                    return ins

                def steps(g, first, last=False):
                    for k in range(2 * T):
                        s = k // T
                        if norm and not (last and s == 1):
                            norm_line(g + s + 1, 1 - s, k % T)
                        if k % T == 0 and not first:
                            act.wait_ge(stored[s], 8 * STORES * g)
                        for b in range(B):
                            act.wait_ge(state_done[b], T * g + k + 1)
                            copy(s, k % T, b, k % 2).then_inc(copied[b], 1)

                act.wait_ge(cleared, 1)
                if norm:
                    for k in range(T):
                        norm_line(0, 0, k)
                steps(0, True)
                with act.Fori(1, G // 2 - 1) as i:
                    steps(2 * i, False)
                steps(G - 2, False, last=True)


def final_sum(nc, sem, x1_rows, l_cols, out):
    with ExitStack() as ctx:
        def sb(name, shape):
            return ctx.enter_context(nc.sbuf_tensor(name, shape, F32))

        res = sb("fin_res", [PP, 2, NP, W])
        lt = sb("fin_l", [PP, 2, G, NP, T])
        o_t = sb("fin_out", [PP, 2, NP, W])
        landed = [sem("fin_in0"), sem("fin_in1")]
        added = sem("fin_added")
        stored = [sem("fin_stored0"), sem("fin_stored1")]
        with nc.Block() as block:
            @block.sync
            def _(sp):
                def load(g, b):
                    sp.dma_start(res[:, b], x1_rows[b, bass.ds(g, 1)].rearrange("g p h w -> (g p) h w")).then_inc(landed[b], 16)
                    sp.dma_start(lt[:, b].rearrange("p c h t -> p c (h t)"),
                                 l_cols[:, :, b, bass.ds(NP * g, NP)].rearrange("c p h t -> p c (h t)")).then_inc(landed[b], 16)

                for b in range(B):
                    load(0, b)
                with sp.Fori(1, G) as g:
                    for b in range(B):
                        sp.wait_ge(added, 2 * g - 1 + b)
                        load(g, b)

            @block.vector
            def _(v):
                def group(g, first):
                    for b in range(B):
                        v.wait_ge(landed[b], 32 * g + 32)
                        if not first:
                            v.wait_ge(stored[b], 32 * g)
                        nc.vector.tensor_tensor(o_t[:, b].rearrange("p h (c t) -> p h c t", t=T),
                                                res[:, b].rearrange("p h (c t) -> p h c t", t=T),
                                                lt[:, b].rearrange("p c h t -> p h c t"), ALU.add).then_inc(added, 1)

                group(0, True)
                with v.Fori(1, G) as g:
                    group(g, False)

            @block.scalar
            def _(act):
                with act.Fori(0, G) as g:
                    for b in range(B):
                        act.wait_ge(added, 2 * g + b + 1)
                        dst = out[b].rearrange("c (m two) w -> two c m w", two=2)
                        for r in range(2):
                            act.dma_start(dst[r, :, bass.ds(NP * g, NP)], o_t[ODD * r:ODD * r + C, b]).then_inc(stored[b], 16)
                for b in range(B):
                    act.wait_ge(stored[b], 32 * G)


def constants():
    import numpy as np
    c = np.arange(B * C)
    same = (c[:, None] // GROUP == c[None, :] // GROUP).astype(np.float32) / np.float32(GROUP)
    gsel = np.zeros((B * C, B, PP), np.float32)
    g112 = np.zeros((PP, PP), np.float32)
    own = same[:C, :C]
    for r in range(2):
        for b in range(B):
            gsel[b * C:(b + 1) * C, b, ODD * r:ODD * r + C] = own
        for q in range(2):
            g112[ODD * r:ODD * r + C, ODD * q:ODD * q + C] = own / 2
    return {"g96": same, "gsel": gsel, "g112": g112, "ident": np.eye(HD, dtype=np.float32)}


def kernel(**inputs):
    import numpy as np
    import concourse.bacc as bacc
    from concourse.bass_utils import run_bass_kernel_spmd as run

    a = {k: np.asarray(v) for k, v in inputs.items()}
    qkv = a["L0_conv_qkv_w"].reshape(3, HEADS, HC, C)
    dw = a["L0_conv_dw_w"].reshape(3, HEADS, HC, 3, 3)[..., ::-1]
    arrays = {
        "x": a["x"],
        "wqk": qkv[:2].transpose(3, 1, 0, 2).reshape(C, 2 * C),
        "wv": qkv[2].reshape(C, C).T,
        "dwqk": dw[:2].transpose(3, 4, 1, 0, 2).reshape(3, 3, 2 * C),
        "dwv": dw[2].transpose(2, 3, 0, 1).reshape(3, 3, C),
        "projT": a["L0_conv_proj_w"].reshape(C, C).T,
        "temp": a["L0_conv_temperature"].reshape(1, HEADS),
    }
    for way in ("down", "right", "left"):
        arrays[f"{way}_w"] = a[f"L1_conv_{way}_w"].transpose(2, 1, 0)
        arrays[f"{way}_b"] = a[f"L1_conv_{way}_b"].reshape(C, 1)
    arrays.update(constants())
    arrays = {k: np.ascontiguousarray(v) for k, v in arrays.items()}

    nc = bacc.Bacc("TRN2", target_bir_lowering=False, num_devices=1)
    args = {k: nc.dram_tensor(k, v.shape, mybir.dt.from_np(v.dtype), kind="ExternalInput").ap() for k, v in arrays.items()}
    out = nc.dram_tensor("out", (B, C, H, W), F32, kind="ExternalOutput").ap()
    program(nc, out=out, **args)
    r = run(nc, [arrays], core_ids=[0])
    return r.results[0]["out"]
```

```python
from contextlib import ExitStack

import concourse.bass as bass
from concourse import mybir

F32 = mybir.dt.float32
F32R = mybir.dt.float32r
ALU = mybir.AluOpType
ACT = mybir.ActivationFunctionType
AX = mybir.AxisListType

B, C, H, W = 2, 48, 512, 512
HEADS = 8
HC = C // HEADS
N = 4
TOK = W // N
HD = HC * N * N
ODD = 64
PP = ODD + C
T = 16
G = H // T
NP = T // 2
NQ = NP + 1
NB = T // N
W2 = W // 2
K = 5
GN_EPS = 1e-5
WAYS = ("down", "up", "right", "left")
GROUP = C // 16
CFG = 4


def flat(ap):
    return ap.rearrange("p a b -> p (a b)")


def program(nc, x, wqkv, dwqkv, projT, temp, down_w, down_b, right_w, right_b, left_w, left_b,
            g96, gsel, g112, ident, out):
    def dram(name, shape):
        return nc.dram_tensor(name, shape, F32).ap()

    v_blocks = dram("v_blocks", (B, G, HD, HEADS, NB * TOK))
    x1_scan = dram("x1_scan", (G, PP, T, B, W2))
    x1_rows = dram("x1_rows", (B, G, PP, NP, W))
    d_rows = dram("d_rows", (G, PP, T, B, W2))
    u_cols = dram("u_cols", (G, PP, B, H // 2, T))
    r_cols = dram("r_cols", (G, PP, T, B, H // 2))
    l_cols = dram("l_cols", (G, PP, B, H // 2, T))

    with ExitStack() as whole:
        def sem(name):
            return whole.enter_context(nc.semaphore(name))

        def keep(name, shape, dt=F32):
            return whole.enter_context(nc.sbuf_tensor(name, shape, dt))

        w_high = keep("w_high", [PP, CFG, 3, 3 * C], F32R)
        w_low = keep("w_low", [PP, CFG, 3, 3 * C], F32R)
        gn0_scale = keep("gn0_scale", [PP, B])
        gn0_bias = keep("gn0_bias", [PP, B])
        top_scale = keep("top_scale", [PP, B, G])
        top_bias = keep("top_bias", [PP, B, G])
        end_scale = keep("end_scale", [PP, B, G])
        end_bias = keep("end_bias", [PP, B, G])
        attT = keep("attT", [HD, B, HEADS, HD])
        x1_stats = keep("x1_stats", [PP, B, G * NP, 6])
        gn1_scale = keep("gn1_scale", [PP, B])
        gn1_bias = keep("gn1_bias", [PP, B])
        g112_sb = keep("g112_sb", [PP, PP])
        eye = keep("eye", [TOK, TOK])

        setup_and_stats(nc, sem, x, wqkv, dwqkv, g96, gsel, g112, ident, w_high, w_low, g112_sb, eye,
                        gn0_scale, gn0_bias, top_scale, top_bias, end_scale, end_bias)
        norm0 = (gn0_scale, gn0_bias, top_scale, top_bias, end_scale, end_bias)
        attention(nc, sem, x, w_high, w_low, norm0, temp, eye, v_blocks, attT)
        for b in range(B):
            mix_values(nc, sem, b, x, projT, eye, attT, v_blocks, x1_scan, x1_rows, x1_stats)
        combine_stats(nc, sem, x1_stats, g112_sb, gn1_scale, gn1_bias)
        steps_sems = [[sem(f"{name}{b}") for b in range(B)] for name in ("conv_done", "state_done", "copied")]
        scan(nc, sem, steps_sems, "down", down_w, down_b, x1_scan, d_rows, gn1_scale, gn1_bias)
        scan(nc, sem, steps_sems, "up", down_w, down_b, d_rows, u_cols, None, None)
        scan(nc, sem, steps_sems, "right", right_w, right_b, u_cols, r_cols, None, None)
        scan(nc, sem, steps_sems, "left", left_w, left_b, r_cols, l_cols, None, None)
        final_sum(nc, sem, x1_rows, l_cols, out)


def inverse_root(nc, link, out, value, root):
    link(nc.vector.reciprocal(out, root))
    link(nc.vector.tensor_tensor(out, out, value, ALU.mult))
    link(nc.vector.tensor_tensor(out, out, root, ALU.add))
    link(nc.vector.tensor_scalar(out, out, 0.5, None, ALU.mult))
    link(nc.vector.reciprocal(out, out))


def setup_and_stats(nc, sem, x, wqkv, dwqkv, g96, gsel, g112, ident, w_high, w_low, g112_sb, eye,
                    gn0_scale, gn0_bias, top_scale, top_bias, end_scale, end_bias):
    CH, FM = 8192, 512
    NCH = H * W // CH
    PER = CH // FM
    BC = B * C
    xv = x.rearrange("b c h w -> (b c) (h w)").rearrange("p (n f) -> p n f", f=CH)
    with ExitStack() as ctx:
        def sb(name, shape):
            return ctx.enter_context(nc.sbuf_tensor(name, shape, F32))

        xs = sb("xs", [BC, 2, CH])
        stats = sb("stats", [BC, NCH * PER, 6])
        mv = sb("mv", [BC, 2])
        diff = sb("diff", [BC, 1])
        var = sb("var", [PP, B])
        root = sb("root", [PP, B])
        g96_sb = sb("g96_sb", [BC, BC])
        gsel_sb = sb("gsel_sb", [BC, B, PP])
        w1 = sb("w1", [PP, 3 * C])
        dw = sb("dw", [PP, CFG, 3, 3 * C])
        dense = sb("dense", [PP, CFG, 3, 3 * C])
        ps_mean = ctx.enter_context(nc.psum_tensor("ps_mean", [BC, 512], F32))
        ps_sel = ctx.enter_context(nc.psum_tensor("ps_sel", [PP, 512], F32))

        cleared, params = sem("cleared"), sem("params")
        chunk = [sem("chunk0"), sem("chunk1")]
        chunk_used = [sem("chunk_used0"), sem("chunk_used1")]
        dv_step = sem("setup_dve")
        mean_ready, group_mean, mv_ready, group_mv = sem("mean_ready"), sem("group_mean"), sem("mv_ready"), sem("group_mv")
        var_ready, root_ready = sem("var_ready"), sem("root_ready")
        NPARAM = 4 + 2 + 6

        with nc.Block() as block:
            @block.sync
            def _(sp):
                sp.dma_start(xs[:, 0], xv[:, 0]).then_inc(chunk[0], 16)
                sp.dma_start(xs[:, 1], xv[:, 1]).then_inc(chunk[1], 16)
                sp.dma_start(g96_sb[:], g96).then_inc(params, 16)
                sp.dma_start(gsel_sb[:], gsel).then_inc(params, 16)
                sp.dma_start(g112_sb[:], g112).then_inc(params, 16)
                sp.dma_start(eye[:], ident).then_inc(params, 16)
                sp.wait_ge(cleared, 1)
                for r in range(2):
                    half = slice(ODD * r, ODD * r + C)
                    sp.dma_start(w1[half, :], wqkv).then_inc(params, 16)
                for cfg, r, ty in ((0, 0, 0), (0, 1, 1), (1, 0, 2), (2, 1, 0), (3, 0, 1), (3, 1, 2)):
                    half = slice(ODD * r, ODD * r + C)
                    sp.dma_start(dw[half, cfg], dwqkv[ty].unsqueeze(0).broadcast_to([C, 3, 3 * C])).then_inc(params, 16)
                with sp.Fori(1, NCH // 2) as i:
                    for s in range(2):
                        sp.wait_ge(chunk_used[s], i)
                        sp.dma_start(xs[:, s], xv[:, bass.ds(2 * i + s, 1)]).then_inc(chunk[s], 16)

            @block.vector
            def _(v):
                nc.vector.memset(w1[:], 0.0)
                nc.vector.memset(dw[:], 0.0).then_inc(cleared, 1)
                with v.Fori(0, NCH // 2) as i:
                    for s in range(2):
                        v.wait_ge(chunk[s], 16 * i + 16)
                        for j in range(PER):
                            last = nc.vector.bn_stats(stats[:, bass.ds((2 * i + s) * PER + j, 1), :],
                                                      xs[:, s, j * FM:(j + 1) * FM])
                        last.then_inc(chunk_used[s], 1)
                n = [0]

                def link(ins):
                    n[0] += 1
                    ins.then_inc(dv_step, 1)
                    v.wait_ge(dv_step, n[0])

                v.wait_ge(chunk_used[1], NCH // 2)
                link(nc.vector.bn_aggr(mv[:], stats[:]))
                nc.vector.tensor_copy(diff[:], mv[:, 0:1]).then_inc(mean_ready, 1)
                v.wait_ge(group_mean, 1)
                link(nc.vector.tensor_tensor(diff[:], mv[:, 0:1], ps_mean[:, 0:1], ALU.subtract))
                link(nc.vector.tensor_tensor(diff[:], diff[:], diff[:], ALU.mult))
                nc.vector.tensor_tensor(mv[:, 1:2], mv[:, 1:2], diff[:], ALU.add).then_inc(mv_ready, 1)
                v.wait_ge(group_mv, 1)
                sel = ps_sel[:, 0:2 * B].rearrange("p (b two) -> p b two", two=2)
                nc.vector.tensor_scalar(var[:], sel[:, :, 1], GN_EPS, None, ALU.add).then_inc(var_ready, 1)
                v.wait_ge(root_ready, 1)
                inverse_root(nc, link, gn0_scale[:], var[:], root[:])
                link(nc.vector.scalar_tensor_tensor(gn0_bias[:], sel[:, :, 0], -1.0, gn0_scale[:], ALU.mult, ALU.mult))
                for src, top, end in ((gn0_scale, top_scale, end_scale), (gn0_bias, top_bias, end_bias)):
                    for tab in (top, end):
                        link(nc.vector.tensor_copy(tab[:], src[:].unsqueeze(2).broadcast_to([PP, B, G])))
                    nc.vector.memset(top[0:C, :, 0], 0.0)
                    link(nc.vector.memset(end[ODD:PP, :, G - 1], 0.0))
                v.wait_ge(params, 16 * NPARAM)
                for cfg in range(CFG):
                    for tx in range(3):
                        ins = nc.vector.tensor_tensor(dense[:, cfg, tx], dw[:, cfg, tx], w1[:], ALU.mult)
                link(ins)
                link(nc.vector.tensor_copy(w_high[:], dense[:]))
                link(nc.vector.tensor_tensor(w_low[:], dense[:], w_high[:], ALU.subtract))

            @block.scalar
            def _(act):
                act.wait_ge(var_ready, 1)
                nc.scalar.activation(root[:], var[:], ACT.Sqrt).then_inc(root_ready, 1)

            @block.tensor
            def _(pe):
                pe.wait_ge(params, 16 * NPARAM)
                pe.wait_ge(mean_ready, 1)
                nc.tensor.matmul(ps_mean[:, 0:1], g96_sb[:], diff[:], start=True, stop=True).then_inc(group_mean, 1)
                pe.wait_ge(mv_ready, 1)
                for b in range(B):
                    last = nc.tensor.matmul(ps_sel[:, 2 * b:2 * b + 2], gsel_sb[:, b], mv[:], start=True, stop=True)
                last.then_inc(group_mv, 1)


def load_pairs(eng, x, b, dst, g, landed, top=False, end=False):
    rows = x[b].rearrange("c (m two) w -> two c m w", two=2)
    a = 1 if top else 0
    e = NQ - 1 if end else NQ
    if top or end:
        eng.dma_start(dst[0:C, a:NQ], rows[1, :, NP * g - 1 + a:NP * g - 1 + NQ]).then_inc(landed, 16)
        eng.dma_start(dst[ODD:PP, 0:e], rows[0, :, NP * g:NP * g + e]).then_inc(landed, 16)
    else:
        eng.dma_start(dst[0:C, :], rows[1, :, bass.ds(NP * g - 1, NQ)]).then_inc(landed, 16)
        eng.dma_start(dst[ODD:PP, :], rows[0, :, bass.ds(NP * g, NQ)]).then_inc(landed, 16)


def norm_factors(norm0, b, g, q):
    gn0_scale, gn0_bias, top_scale, top_bias, end_scale, end_bias = norm0
    if q == 0:
        return top_scale[:, b, bass.ds(g, 1)], top_bias[:, b, bass.ds(g, 1)]
    if q == NQ - 1:
        return end_scale[:, b, bass.ds(g, 1)], end_bias[:, b, bass.ds(g, 1)]
    return gn0_scale[:, b:b + 1], gn0_bias[:, b:b + 1]


def attention(nc, sem, x, w_high, w_low, norm0, temp, eye, v_blocks, attT):
    HQ = 2 * HEADS
    QKV = 3 * C
    with ExitStack() as ctx:
        def sb(name, shape, dt=F32):
            return ctx.enter_context(nc.sbuf_tensor(name, shape, dt))

        sumsq = sb("sumsq", [TOK, B, HQ, HD])
        ones = sb("ones", [TOK, HD])
        gram_sb = sb("gram_sb", [HD, B, HEADS, HD])

        with ExitStack() as inner:
            def sbi(name, shape, dt=F32):
                return inner.enter_context(nc.sbuf_tensor(name, shape, dt))

            def psum(name, shape):
                return inner.enter_context(nc.psum_tensor(name, shape, F32))

            raw = sbi("raw", [PP, 2, NQ, W])
            x_high = sbi("x_high", [PP, 2, NQ, N, TOK + 2], F32R)
            x_low = sbi("x_low", [PP, 2, NQ, N, TOK + 2], F32R)
            qk = sbi("qk", [TOK, 2, HQ, N * N, HC])
            vt = sbi("vt", [TOK, 2, HEADS, N * N, HC])
            v_out = sbi("v_out", [HD, 2, HEADS, NB // 2, TOK])
            sq = sbi("sq", [TOK, HQ * HD])
            zero_row = sbi("zero_row", [TOK, 512])
            conv_ps = psum("conv_ps", [TOK, 2, N, 256])
            gram_ps = psum("gram_ps", [HD, 2, 512])
            vt_ps = psum("vt_ps", [HD, HEADS, TOK])

            tiles_clear, zero_ready, sums_clear = sem("tiles_clear"), sem("zero_ready"), sem("sums_clear")

            def per_batch(name):
                return [sem(f"{name}_b{b}") for b in range(B)]

            raw_in = [[sem(f"qk_raw_in_b{b}_{s}") for s in range(2)] for b in range(B)]
            normed, high_ready, low_ready = per_batch("normed"), per_batch("high_ready"), per_batch("low_ready")
            conv_done, act_moved, dve_moved = per_batch("conv_done"), per_batch("act_moved"), per_batch("dve_moved")
            gram_done, sq_ready, squared = per_batch("gram_done"), per_batch("sq_ready"), per_batch("squared")
            vt_done, vt_moved, gram_saved = per_batch("vt_done"), per_batch("vt_moved"), per_batch("gram_saved")
            v_stored = [[sem(f"v_stored_b{b}_{s}") for s in range(2)] for b in range(B)]

            def move(engine, slot, dy):
                src = conv_ps[:, dy % 2]
                engine(qk[:, slot, :, N * dy:N * dy + N, :], src[:, :, 0:2 * C].rearrange("p d (h c) -> p h d c", c=HC))
                return engine(vt[:, slot, :, N * dy:N * dy + N, :], src[:, :, 2 * C:QKV].rearrange("p d (h c) -> p h d c", c=HC))

            def pairs_at(slot):
                return [q for q in (2 * slot, 2 * slot + 1) if 0 <= q < NQ]

            with nc.Block() as block:
                @block.gpsimd
                def _(pool):
                    nc.gpsimd.memset(raw[:], 0.0)
                    nc.gpsimd.memset(x_high[:].bitcast(F32), 0.0)
                    nc.gpsimd.memset(x_low[:].bitcast(F32), 0.0).then_inc(tiles_clear, 1)

                @block.sync
                def _(sp):
                    sp.wait_ge(tiles_clear, 1)
                    for b in range(B):
                        for s in range(2):
                            if b:
                                sp.wait_ge(low_ready[b - 1], G - 1 + s)
                            load_pairs(sp, x, b, raw[:, s], s, raw_in[b][s], top=s == 0)
                        with sp.Fori(1, G // 2 - 1) as i:
                            for s in range(2):
                                sp.wait_ge(low_ready[b], 2 * i + s - 1)
                                load_pairs(sp, x, b, raw[:, s], 2 * i + s, raw_in[b][s])
                        for s in range(2):
                            sp.wait_ge(low_ready[b], G - 3 + s)
                            load_pairs(sp, x, b, raw[:, s], G - 2 + s, raw_in[b][s], end=s == 1)

                @block.scalar
                def _(act):
                    def high(b, g, s, q):
                        act.wait_ge(normed[b], NQ * g + q + 1)
                        nc.scalar.copy(x_high[:, s, q, :, 1:TOK + 1],
                                       raw[:, s, q].rearrange("p (j m) -> p m j", m=N)).then_inc(high_ready[b], 1)

                    def v_block(b, n, g, i):
                        half = i // 2
                        if i % 2 == 0 and not (isinstance(g, int) and g == 0):
                            act.wait_ge(v_stored[b][half], 16 * g)
                        act.wait_ge(vt_done[b], n + 1)
                        nc.scalar.copy(v_out[:, half, :, i % 2, :], vt_ps[:]).then_inc(vt_moved[b], 1)
                        if i % 2:
                            act.wait_ge(vt_moved[b], n + 1)
                            act.dma_start(v_blocks[b, bass.ds(g, 1), :, :, half * 2 * TOK:(half + 1) * 2 * TOK]
                                          .rearrange("g p h n -> (g p) h n"),
                                          v_out[:, half].rearrange("p h i n -> p h (i n)")).then_inc(v_stored[b][half], 16)

                    def group(b, g, s, first, last_group=False):
                        for i in range(NB):
                            n = NB * g + i
                            for dy in (0, 2):
                                if not last_group:
                                    slot = 2 * i + dy // 2 - 1
                                    if slot == 0 and not first:
                                        act.wait_ge(conv_done[b], N * NB * g)
                                    for q in pairs_at(slot):
                                        high(b, g + 1, 1 - s, q)
                                if not (first and i < 2):
                                    act.wait_ge(gram_done[b], n - 1)
                                    act.wait_ge(squared[b], n - 1)
                                    act.wait_ge(vt_done[b], n - 1)
                                act.wait_ge(conv_done[b], N * n + dy + 1)
                                move(nc.scalar.copy, i % 2, dy).then_inc(act_moved[b], 1)
                                if dy == 2 and not (first and i == 0):
                                    v_block(b, n - 1, g if i else g - 1, (i - 1) % NB)

                    act.wait_ge(tiles_clear, 1)
                    for b in range(B):
                        if b:
                            act.wait_ge(conv_done[b - 1], N * NB * G)
                            act.wait_ge(gram_done[b - 1], NB * G)
                            act.wait_ge(squared[b - 1], NB * G)
                            for s in range(2):
                                act.wait_ge(v_stored[b - 1][s], 16 * G)
                        for q in range(NQ):
                            high(b, 0, 0, q)
                        group(b, 0, 0, True)
                        group(b, 1, 1, False)
                        with act.Fori(1, G // 2 - 1) as i:
                            group(b, 2 * i, 0, False)
                            group(b, 2 * i + 1, 1, False)
                        group(b, G - 2, 0, False)
                        group(b, G - 1, 1, False, last_group=True)
                        v_block(b, NB * G - 1, G - 1, NB - 1)
                    for s in range(2):
                        act.wait_ge(v_stored[B - 1][s], 16 * G)

                @block.tensor
                def _(pe):
                    def gram_block(b, n, slot):
                        pe.wait_ge(act_moved[b], 2 * n + 2)
                        pe.wait_ge(dve_moved[b], 2 * n + 2)
                        for h in range(HEADS):
                            last = nc.tensor.matmul(gram_ps[:, h // 4, (h % 4) * HD:(h % 4 + 1) * HD],
                                                    flat(qk[:, slot, 2 * h]), flat(qk[:, slot, 2 * h + 1]),
                                                    start=False, stop=False, skip_group_check=True)
                        last.then_inc(gram_done[b], 1)

                    def v_transposes(b, n, slot):
                        for h in range(HEADS):
                            last = nc.tensor.transpose(vt_ps[:, h], flat(vt[:, slot, h]), eye[:])
                        last.then_inc(vt_done[b], 1)

                    def group(b, g, s, first):
                        pe.wait_ge(low_ready[b], g + 1)
                        for i in range(NB):
                            n = NB * g + i
                            for dy in range(N):
                                if not (first and i == 0 and dy < 2):
                                    if dy % 2 == 0:
                                        pe.wait_ge(act_moved[b], 2 * n + dy // 2)
                                    else:
                                        pe.wait_ge(dve_moved[b], 2 * n + dy // 2)
                                fresh = [True, True]
                                for col, lo, hi in ((0, 0, 1), (3, 2, 3), (1, 0, 1), (1, 2, 2), (2, 1, 1), (2, 2, 3),
                                                    (-1, 0, 0), (N, 3, 3)):
                                    start = col // N + 1
                                    for pair in range(2):
                                        cfg = pair + 2 * (dy % 2)
                                        at = (slice(None), s, 2 * i + dy // 2 + pair, col % N, slice(start, start + TOK))
                                        taps = (slice(None), cfg, slice(lo - col + 1, hi - col + 2))
                                        for xs, ws in ((x_high, w_high), (x_high, w_low), (x_low, w_high)):
                                            final = col in (-1, N) and pair == 1 and xs is x_low
                                            last = nc.tensor.matmul(conv_ps[:, dy % 2, lo:hi + 1, 0:QKV], xs[at], ws[taps],
                                                                    start=fresh[lo // 2], stop=final, skip_group_check=True)
                                            fresh[lo // 2] = False
                                last.then_inc(conv_done[b], 1)
                                if dy == 0 and not (first and i == 0):
                                    gram_block(b, n - 1, (i - 1) % 2)
                                    if not (first and i == 1):
                                        pe.wait_ge(vt_moved[b], n - 1)
                                    v_transposes(b, n - 1, (i - 1) % 2)

                    pe.wait_ge(zero_ready, 1)
                    for b in range(B):
                        if b:
                            pe.wait_ge(gram_saved[b - 1], 1)
                            pe.wait_ge(act_moved[b - 1], 2 * NB * G)
                            pe.wait_ge(dve_moved[b - 1], 2 * NB * G)
                            pe.wait_ge(vt_moved[b - 1], NB * G)
                        for half in range(2):
                            nc.tensor.matmul(gram_ps[:, half], zero_row[:, 0:HD], zero_row[:], start=True, stop=False,
                                             skip_group_check=True)
                        group(b, 0, 0, True)
                        group(b, 1, 1, False)
                        with pe.Fori(1, G // 2) as i:
                            group(b, 2 * i, 0, False)
                            group(b, 2 * i + 1, 1, False)
                        gram_block(b, NB * G - 1, (NB - 1) % 2)
                        pe.wait_ge(vt_moved[b], NB * G - 1)
                        v_transposes(b, NB * G - 1, (NB - 1) % 2)

                @block.vector
                def _(v):
                    nc.vector.memset(zero_row[:], 0.0).then_inc(zero_ready, 1)
                    nc.vector.memset(ones[:], 1.0)
                    nc.vector.memset(sumsq[:], 0.0).then_inc(sums_clear, 1)
                    v.wait_ge(sums_clear, 1)

                    def norm(b, g, s, q):
                        scale, bias = norm_factors(norm0, b, g, q)
                        nc.vector.tensor_scalar(raw[:, s, q], raw[:, s, q], scale, bias, ALU.mult, ALU.add).then_inc(normed[b], 1)

                    def low(b, g, s, q):
                        v.wait_ge(high_ready[b], NQ * g + q + 1)
                        ins = nc.vector.tensor_tensor(x_low[:, s, q, :, 1:TOK + 1],
                                                      raw[:, s, q].rearrange("p (j m) -> p m j", m=N),
                                                      x_high[:, s, q, :, 1:TOK + 1], ALU.subtract)
                        if q == NQ - 1:
                            ins.then_inc(low_ready[b], 1)

                    def group(b, g, s, first, last_group=False):
                        for i in range(NB):
                            n = NB * g + i
                            if not (first and i < 2):
                                v.wait_ge(gram_done[b], n - 1)
                                v.wait_ge(vt_done[b], n - 1)
                            for dy in (1, 3):
                                slot = 2 * i + dy // 2
                                if not last_group:
                                    if slot == 0:
                                        v.wait_ge(raw_in[b][1 - s], 32 if first else 16 * (g + 1 - (1 - s)) + 32)
                                    for q in pairs_at(slot):
                                        norm(b, g + 1, 1 - s, q)
                                v.wait_ge(conv_done[b], N * n + dy + 1)
                                move(nc.vector.tensor_copy, i % 2, dy).then_inc(dve_moved[b], 1)
                                if not last_group:
                                    for q in pairs_at(slot - 2):
                                        low(b, g + 1, 1 - s, q)
                            v.wait_ge(act_moved[b], 2 * n + 2)
                            v.wait_ge(dve_moved[b], 2 * n + 2)
                            all_qk = qk[:, i % 2].rearrange("p h s c -> p (h s c)")
                            nc.vector.tensor_tensor(sq[:], all_qk, all_qk, ALU.mult).then_inc(sq_ready[b], 1)
                            v.wait_ge(sq_ready[b], n + 1)
                            if not (first and i == 0):
                                v.wait_ge(squared[b], n)
                            sums = sumsq[:, b].rearrange("p h d -> p (h d)")
                            nc.vector.tensor_tensor(sums, sums, sq[:], ALU.add).then_inc(squared[b], 1)

                    for b in range(B):
                        v.wait_ge(raw_in[b][0], 32)
                        for q in range(NQ):
                            norm(b, 0, 0, q)
                        for q in range(NQ):
                            low(b, 0, 0, q)
                        group(b, 0, 0, True)
                        group(b, 1, 1, False)
                        with v.Fori(1, G // 2 - 1) as i:
                            group(b, 2 * i, 0, False)
                            group(b, 2 * i + 1, 1, False)
                        group(b, G - 2, 0, False)
                        group(b, G - 1, 1, False, last_group=True)
                        v.wait_ge(gram_done[b], NB * G)
                        nc.vector.tensor_copy(gram_sb[:, b].rearrange("p (f h) d -> p f (h d)", f=2),
                                              gram_ps[:, :, 0:4 * HD]).then_inc(gram_saved[b], 1)

        softmax(nc, sem, sumsq, ones, gram_sb, temp, eye, attT)


def softmax(nc, sem, sumsq, ones, gram_sb, temp, eye, attT):
    HQ = 2 * HEADS
    with ExitStack() as ctx:
        def sb(name, shape):
            return ctx.enter_context(nc.sbuf_tensor(name, shape, F32))

        temp_sb = sb("temp_sb", [HD, HEADS])
        rnorm = sb("rnorm", [HD, B, HQ])
        norm2 = sb("norm2", [HD, HQ])
        norm = sb("norm", [HD, HQ])
        diag = sb("diag", [HD, HEADS, HD])
        att = sb("att", [HD, HEADS, HD])
        prob = sb("prob", [HD, HEADS, HD])
        top = sb("top", [HD, HEADS])
        total = sb("total", [HD, HEADS])
        ps = ctx.enter_context(nc.psum_tensor("att_ps", [HD, 2, 512], F32))
        params, norms, scaled = sem("att_params"), sem("norms"), sem("diag_ready")
        spread, negmax, exped, probs = sem("spread"), sem("negmax"), sem("exped"), sem("probs")
        turned, turned_moved, step = sem("turned"), sem("turned_moved"), sem("att_step")
        norm2_ready, norm_ready = sem("norm2_ready"), sem("norm_ready")

        with nc.Block() as block:
            @block.sync
            def _(sp):
                sp.dma_start(temp_sb[:], temp.broadcast_to([HD, HEADS])).then_inc(params, 16)

            @block.vector
            def _(v):
                n = [0]

                def link(ins):
                    n[0] += 1
                    ins.then_inc(step, 1)
                    v.wait_ge(step, n[0])

                v.wait_ge(params, 16)
                for b in range(B):
                    v.wait_ge(norms, b + 1)
                    nc.vector.tensor_scalar(norm2[:], ps[:, 0, 0:HQ], 1e-24, None, ALU.max).then_inc(norm2_ready, 1)
                    v.wait_ge(norm_ready, b + 1)
                    inverse_root(nc, link, rnorm[:, b], norm2[:], norm[:])
                    rk = rnorm[:, b].rearrange("p (h two) -> p h two", two=2)[:, :, 1]
                    link(nc.vector.tensor_tensor(rk, rk, temp_sb[:], ALU.mult))
                    for h in range(HEADS):
                        ins = nc.vector.tensor_scalar(diag[:, h], eye[0:HD, 0:HD], rnorm[:, b, 2 * h + 1:2 * h + 2], None, ALU.mult)
                    ins.then_inc(scaled, 1)
                    v.wait_ge(spread, b + 1)
                    for h in range(HEADS):
                        ins = nc.vector.tensor_scalar(att[:, h], gram_sb[:, b, h], rnorm[:, b, 2 * h:2 * h + 1], None, ALU.mult)
                    link(ins)
                    halves = att[:].rearrange("p (f h) d -> p f (h d)", f=2)
                    link(nc.vector.tensor_tensor(halves, halves, ps[:, :, 0:4 * HD], ALU.mult))
                    link(nc.vector.tensor_reduce(top[:], att[:], AX.X, ALU.max))
                    nc.vector.tensor_scalar(top[:], top[:], -1.0, None, ALU.mult).then_inc(negmax, 1)
                    v.wait_ge(exped, HEADS * (b + 1))
                    link(nc.vector.reciprocal(total[:], total[:]))
                    for h in range(HEADS):
                        ins = nc.vector.tensor_scalar(prob[:, h], prob[:, h], total[:, h:h + 1], None, ALU.mult)
                    ins.then_inc(probs, 1)
                    v.wait_ge(turned, b + 1)
                    nc.vector.tensor_copy(attT[:, b].rearrange("p (f h) d -> p f (h d)", f=2),
                                          ps[:, :, 0:4 * HD]).then_inc(turned_moved, 1)

            @block.scalar
            def _(act):
                for b in range(B):
                    act.wait_ge(norm2_ready, b + 1)
                    nc.scalar.activation(norm[:], norm2[:], ACT.Sqrt).then_inc(norm_ready, 1)
                    act.wait_ge(negmax, b + 1)
                    for h in range(HEADS):
                        nc.scalar.activation(prob[:, h], att[:, h], ACT.Exp, bias=top[:, h:h + 1],
                                             accum_out=total[:, h:h + 1]).then_inc(exped, 1)

            @block.tensor
            def _(pe):
                for b in range(B):
                    if b:
                        pe.wait_ge(turned_moved, b)
                    for k in range(HQ):
                        last = nc.tensor.matmul(ps[:, 0, k:k + 1], sumsq[:, b, k], ones[:, 0:1], start=True, stop=True)
                    last.then_inc(norms, 1)
                    pe.wait_ge(scaled, b + 1)
                    for half in range(2):
                        last = nc.tensor.matmul(ps[:, half, 0:4 * HD], ones[0:HD, :],
                                                flat(diag[:, 4 * half:4 * half + 4]), start=True, stop=True)
                    last.then_inc(spread, 1)
                    pe.wait_ge(probs, b + 1)
                    for h in range(HEADS):
                        last = nc.tensor.transpose(ps[:, h // 4, (h % 4) * HD:(h % 4 + 1) * HD], prob[:, h], eye[0:HD, 0:HD])
                    last.then_inc(turned, 1)


def mix_values(nc, sem, b, x, projT, eye, attT, v_blocks, x1_scan, x1_rows, x1_stats):
    NM = N * N // 2
    NBANK = 4
    with ExitStack() as ctx:
        def sb(name, shape):
            return ctx.enter_context(nc.sbuf_tensor(f"{name}_b{b}", shape, F32))

        def s_(name):
            return sem(f"{name}_b{b}")

        res = sb("res", [PP, 2, NP, W])
        v_in = sb("v_in", [HD, 2, HEADS, NB, TOK])
        mixed = sb("mixed", [TOK, 2, N * N, ODD])
        turned = sb("turned", [PP, 2, NM, NB, TOK])
        projd = sb("projd", [PP, PP])
        scan_t = sb("scan_t", [PP, 2, T, W2])
        rows_t = sb("rows_t", [PP, 2, NP, W])
        a_ps = ctx.enter_context(nc.psum_tensor(f"a_ps{b}", [TOK, 2, 512], F32))
        t_ps = ctx.enter_context(nc.psum_tensor(f"t_ps{b}", [PP, NM, TOK], F32))
        o_ps = ctx.enter_context(nc.psum_tensor(f"o_ps{b}", [PP, NBANK, 512], F32))
        cleared, proj_in = s_("mix_cleared"), s_("proj_in")
        v_landed, res_landed = [s_("v_landed0"), s_("v_landed1")], [s_("res_landed0"), s_("res_landed1")]
        att_done, act_took, dve_took = s_("att_done"), s_("act_took"), s_("dve_took")
        turn_done, turn_moved, o_done = s_("turn_done"), s_("turn_moved"), s_("o_done")
        summed, rows_done = s_("summed"), s_("rows_done")
        scan_out = [s_("scan_out0"), s_("scan_out1")]
        rows_out = [s_("rows_out0"), s_("rows_out1")]

        def take(engine, half, slot):
            dst = mixed[:, slot, :, 4 * HC * half:4 * HC * (half + 1)].rearrange("p s (h c) -> p h s c", c=HC)
            return engine(dst, a_ps[:, half, 0:4 * HD].rearrange("p (h s c) -> p h s c", s=N * N, c=HC))

        with nc.Block() as block:
            @block.sync
            def _(sp):
                def load_v(g, s):
                    sp.dma_start(v_in[:, s].rearrange("p h i n -> p h (i n)"),
                                 v_blocks[b, bass.ds(g, 1)].rearrange("g p h n -> (g p) h n")).then_inc(v_landed[s], 16)

                def load_res(g, s):
                    rows = x[b].rearrange("c (m two) w -> two c m w", two=2)
                    for r in range(2):
                        sp.dma_start(res[ODD * r:ODD * r + C, s], rows[r, :, bass.ds(NP * g, NP)]).then_inc(res_landed[s], 16)

                load_v(0, 0)
                sp.wait_ge(cleared, 1)
                for q in range(2):
                    sp.dma_start(projd[ODD * q:ODD * q + C, ODD * q:ODD * q + C], projT).then_inc(proj_in, 16)
                load_res(0, 0)
                load_v(1, 1)
                load_res(1, 1)
                with sp.Fori(1, G // 2) as i:
                    for s in range(2):
                        sp.wait_ge(att_done, NB * (2 * i + s - 1))
                        load_v(2 * i + s, s)
                        sp.wait_ge(summed, NM * (2 * i + s - 1))
                        load_res(2 * i + s, s)

            @block.tensor
            def _(pe):
                def project(g, s, ms, first):
                    for m in ms:
                        if not (first and m < NBANK):
                            pe.wait_ge(summed, NM * g + m - NBANK + 1)
                        nc.tensor.matmul(o_ps[:, m % NBANK], projd[:], flat(turned[:, s, m]),
                                         start=True, stop=True).then_inc(o_done, 1)

                def turn(n, slot, first):
                    pe.wait_ge(act_took, n + 1)
                    pe.wait_ge(dve_took, n + 1)
                    if not first:
                        pe.wait_ge(turn_moved, n)
                    for m in range(NM):
                        last = nc.tensor.transpose(t_ps[:, m], flat(mixed[:, slot, 2 * m:2 * m + 2])[:, 0:PP], eye[:])
                    last.then_inc(turn_done, 1)

                def group(g, s, first):
                    pe.wait_ge(v_landed[s], 8 * (g - s) + 16)
                    for i in range(NB):
                        n = NB * g + i
                        if not (first and i == 0):
                            pe.wait_ge(act_took, n)
                            pe.wait_ge(dve_took, n)
                        for h in range(HEADS):
                            last = nc.tensor.matmul(a_ps[:, h // 4, (h % 4) * HD:(h % 4 + 1) * HD], v_in[:, s, h, i, :],
                                                    attT[:, b, h], start=True, stop=True)
                        last.then_inc(att_done, 1)
                        if i:
                            turn(n - 1, (i - 1) % 2, first and i == 1)
                        if not first:
                            if i == 0:
                                pe.wait_ge(turn_moved, n)
                            project(g - 1, 1 - s, (2 * i, 2 * i + 1), isinstance(g, int))
                    turn(NB * g + NB - 1, (NB - 1) % 2, False)

                pe.wait_ge(proj_in, 32)
                group(0, 0, True)
                group(1, 1, False)
                with pe.Fori(1, G // 2) as i:
                    group(2 * i, 0, False)
                    group(2 * i + 1, 1, False)
                pe.wait_ge(turn_moved, NB * G)
                project(G - 1, 1, range(NM), False)

            @block.scalar
            def _(act):
                def turned_out(n, s, i):
                    act.wait_ge(turn_done, n + 1)
                    nc.scalar.copy(turned[:, s, :, i, :], t_ps[:]).then_inc(turn_moved, 1)

                def rows(g, s, dy):
                    act.wait_ge(summed, NM * g + 2 * dy + 2)
                    for q in range(2):
                        ins = nc.scalar.copy(
                            rows_t[ODD * (dy % 2):ODD * (dy % 2) + C, s, dy // 2:NP:2, q:W:2],
                            scan_t[ODD * q:ODD * q + C, s, dy:T:N, :])
                    ins.then_inc(rows_done, 1)

                def store(g, s):
                    act.wait_ge(rows_done, N * g + N)
                    act.dma_start(x1_scan[bass.ds(g, 1), :, :, b].rearrange("g p t w -> (g p) t w"), scan_t[:, s]).then_inc(scan_out[s], 16)
                    act.dma_start(x1_rows[b, bass.ds(g, 1)].rearrange("g p t w -> (g p) t w"), rows_t[:, s]).then_inc(rows_out[s], 16)

                def group(g, s, first, free):
                    for i in range(NB):
                        n = NB * g + i
                        if not (first and i < 2):
                            act.wait_ge(turn_done, n - 1)
                        act.wait_ge(att_done, n + 1)
                        take(nc.scalar.copy, 0, i % 2).then_inc(act_took, 1)
                        if i:
                            if i == 1 and not (isinstance(g, int) and g < 2):
                                act.wait_ge(o_done, NM * (g - 1))
                            turned_out(n - 1, s, i - 1)
                        if not first:
                            if i == 0 and free is not None:
                                act.wait_ge(rows_out[1 - s], free)
                            rows(g - 1, 1 - s, i)
                    turned_out(NB * g + NB - 1, s, NB - 1)
                    if not first:
                        store(g - 1, 1 - s)

                act.wait_ge(cleared, 1)
                group(0, 0, True, None)
                group(1, 1, False, None)
                group(2, 0, False, None)
                group(3, 1, False, 16)
                with act.Fori(2, G // 2) as i:
                    group(2 * i, 0, False, 16 * i - 16)
                    group(2 * i + 1, 1, False, 16 * i)
                act.wait_ge(rows_out[1], 16 * (G // 2 - 1))
                for dy in range(N):
                    rows(G - 1, 1, dy)
                store(G - 1, 1)
                for s in range(2):
                    act.wait_ge(scan_out[s], 16 * (G // 2))
                    act.wait_ge(rows_out[s], 16 * (G // 2))

            @block.vector
            def _(v):
                nc.vector.memset(projd[:], 0.0)
                nc.vector.memset(mixed[:], 0.0)
                nc.vector.memset(scan_t[:], 0.0)
                nc.vector.memset(rows_t[:], 0.0).then_inc(cleared, 1)
                v.wait_ge(cleared, 1)

                def sums(g, s, dy):
                    r, q0 = dy % 2, dy // 2
                    for dx2 in range(2):
                        m = 2 * dy + dx2
                        v.wait_ge(o_done, NM * g + m + 1)
                        for q in range(2):
                            ins = nc.vector.tensor_tensor(
                                scan_t[ODD * q:ODD * q + C, s, dy:T:N, dx2:W2:2],
                                o_ps[ODD * q:ODD * q + C, m % NBANK].rearrange("p (i j) -> p i j", j=TOK),
                                res[ODD * r:ODD * r + C, s, q0:NP:2, 2 * dx2 + q:W:N], ALU.add)
                        ins.then_inc(summed, 1)
                    v.wait_ge(summed, NM * g + 2 * dy + 2)
                    for half in range(2):
                        at = dy + 2 * N * half
                        nc.vector.bn_stats(x1_stats[:, b, bass.ds(NP * g + 2 * dy + half, 1), :],
                                           scan_t[:, s, at:at + N + 1:N, :])

                def group(g, s, first, free):
                    for i in range(NB):
                        n = NB * g + i
                        if not (first and i < 2):
                            v.wait_ge(turn_done, n - 1)
                        v.wait_ge(att_done, n + 1)
                        take(nc.vector.tensor_copy, 1, i % 2).then_inc(dve_took, 1)
                        if not first:
                            if i == 0:
                                v.wait_ge(res_landed[1 - s], 16 * (g - 1 - (1 - s)) + 32)
                                if free is not None:
                                    v.wait_ge(scan_out[1 - s], free)
                                    v.wait_ge(rows_done, N * (g - 2))
                            sums(g - 1, 1 - s, i)

                group(0, 0, True, None)
                group(1, 1, False, None)
                group(2, 0, False, None)
                group(3, 1, False, 16)
                with v.Fori(2, G // 2) as i:
                    group(2 * i, 0, False, 16 * i - 16)
                    group(2 * i + 1, 1, False, 16 * i)
                v.wait_ge(res_landed[1], 16 * G)
                v.wait_ge(scan_out[1], 16 * (G // 2 - 1))
                v.wait_ge(rows_done, N * (G - 2))
                for dy in range(N):
                    sums(G - 1, 1, dy)


def combine_stats(nc, sem, x1_stats, g112_sb, gn1_scale, gn1_bias):
    with ExitStack() as ctx:
        mean = ctx.enter_context(nc.sbuf_tensor("gn1_mean", [PP, B], F32))
        var = ctx.enter_context(nc.sbuf_tensor("gn1_var", [PP, B], F32))
        mv = ctx.enter_context(nc.sbuf_tensor("gn1_mv", [PP, B, 2], F32))
        off = ctx.enter_context(nc.sbuf_tensor("gn1_off", [PP, B], F32))
        gm = ctx.enter_context(nc.sbuf_tensor("gn1_gm", [PP, B], F32))
        root = ctx.enter_context(nc.sbuf_tensor("gn1_root", [PP, B], F32))
        sum_ready, root_ready = sem("gn1_sum_ready"), sem("gn1_root_ready")
        ps = ctx.enter_context(nc.psum_tensor("gn1_ps", [PP, 2, 512], F32))
        step, mean_ready, group_mean, var_ready, group_var = (
            sem("gn1_step"), sem("gn1_mean_ready"), sem("gn1_group_mean"), sem("gn1_var_ready"), sem("gn1_group_var"))
        with nc.Block() as block:
            @block.vector
            def _(v):
                n = [0]

                def link(ins):
                    n[0] += 1
                    ins.then_inc(step, 1)
                    v.wait_ge(step, n[0])

                for b in range(B):
                    link(nc.vector.bn_aggr(mv[:, b], x1_stats[:, b]))
                nc.vector.tensor_copy(mean[:], mv[:, :, 0]).then_inc(mean_ready, 1)
                v.wait_ge(group_mean, 1)
                link(nc.vector.tensor_copy(gm[:], ps[:, 0, 0:B]))
                link(nc.vector.tensor_tensor(off[:], mean[:], gm[:], ALU.subtract))
                link(nc.vector.tensor_tensor(off[:], off[:], off[:], ALU.mult))
                nc.vector.tensor_tensor(var[:], mv[:, :, 1], off[:], ALU.add).then_inc(var_ready, 1)
                v.wait_ge(group_var, 1)
                nc.vector.tensor_scalar(var[:], ps[:, 1, 0:B], GN_EPS, None, ALU.add).then_inc(sum_ready, 1)
                v.wait_ge(root_ready, 1)
                inverse_root(nc, link, gn1_scale[:], var[:], root[:])
                link(nc.vector.scalar_tensor_tensor(gn1_bias[:], gm[:], -1.0, gn1_scale[:], ALU.mult, ALU.mult))

            @block.scalar
            def _(act):
                act.wait_ge(sum_ready, 1)
                nc.scalar.activation(root[:], var[:], ACT.Sqrt).then_inc(root_ready, 1)

            @block.tensor
            def _(pe):
                pe.wait_ge(mean_ready, 1)
                nc.tensor.matmul(ps[:, 0, 0:B], g112_sb[:], mean[:], start=True, stop=True).then_inc(group_mean, 1)
                pe.wait_ge(var_ready, 1)
                nc.tensor.matmul(ps[:, 1, 0:B], g112_sb[:], var[:], start=True, stop=True).then_inc(group_var, 1)


def scan(nc, sem, steps_sems, way, taps, bias, src, dst, scale1, bias1):
    LP = W2
    n_params = 2 * K + 2 + (way == "up")
    with ExitStack() as ctx:
        def sb(name, shape):
            return ctx.enter_context(nc.sbuf_tensor(f"{way}_{name}", shape, F32))

        def s_(name):
            return sem(f"{way}_{name}")

        u_in = sb("u_in", [PP, 2, T * B * LP])
        o_t = sb("o_t", [PP, 2, T * B * LP])
        state = sb("state", [PP, B, 2, LP + 2])
        w_sb = sb("taps", [PP, 3, PP])
        b_sb = sb("bias", [PP, 1])
        token = sb("token", [1, 3])
        ps = ctx.enter_context(nc.psum_tensor(f"{way}_ps", [PP, B, 512], F32))
        cleared, params = s_("cleared"), s_("params")
        loaded = [s_("loaded0"), s_("loaded1")]
        stored = [s_("stored0"), s_("stored1")]
        conv_done, state_done, copied = steps_sems
        before_here = WAYS.index(way)
        convs0, states0 = (W - 1) * before_here, W * before_here
        norm = scale1 is not None
        normed = s_("normed") if norm else None
        LOADS = 2 if way == "up" else 1
        STORES = 2 if way == "up" else 1

        def line(s, k, b):
            if way == "right":
                return u_in[:, s].rearrange("p (b n t) -> p b n t", b=B, t=T)[:, b, :, k]
            at = k if way == "down" else T - 1 - k
            return u_in[:, s].rearrange("p (t b n) -> p t b n", b=B, t=T)[:, at, b]

        with nc.Block() as block:
            @block.sync
            def _(sp):
                sp.wait_ge(cleared, 1)
                for r in range(2):
                    sp.dma_start(b_sb[ODD * r:ODD * r + C], bias).then_inc(params, 16)
                    for shift in range(3):
                        for q in range(2):
                            k = 2 * (shift - 1) + r - q + K // 2
                            if 0 <= k < K:
                                sp.dma_start(w_sb[ODD * r:ODD * r + C, shift, ODD * q:ODD * q + C],
                                             taps[k]).then_inc(params, 16)

                def one(t, g):
                    return t[bass.ds(g, 1)]

                def load(g, s, first=False, last=False):
                    if way != "up":
                        at = g * -1 + (G - 1) if way == "left" else g
                        tile = one(src, at).rearrange("g p a b c -> (g p) (a b c)")
                        sp.dma_start(u_in[:, s], tile).then_inc(loaded[s], 16)
                        return
                    rows = u_in[:, s].rearrange("p (t x) -> p t x", t=T)
                    here = one(src, g * -1 + (G - 1)).rearrange("g p t b n -> (g p) t (b n)")
                    before = one(src, G - 1 if last else g * -1 + (G - 2)).rearrange("g p t b n -> (g p) t (b n)")
                    if first:
                        sp.dma_start(rows[:, T - 1:T], here[:, T - 1:T]).then_inc(params, 16)
                        sp.dma_start(rows[:, 1:T - 1], here[:, 0:T - 2]).then_inc(loaded[s], 16)
                    else:
                        sp.dma_start(rows[:, 1:T], here[:, 0:T - 1]).then_inc(loaded[s], 16)
                    sp.dma_start(rows[:, 0:1], before[:, T - 1:T]).then_inc(loaded[s], 16)

                def store(g, s):
                    for b in range(B):
                        sp.wait_ge(copied[b], states0 + T * g + T)
                    if way == "up":
                        for b in range(B):
                            tile = o_t[:, s].rearrange("p (b c x) -> p b c x", b=B, c=W // T)[:, b]
                            sp.dma_start(dst[:, :, b, bass.ds(g * -NP + NP * (G - 1), NP)].rearrange("c p h t -> p c (h t)"),
                                         tile).then_inc(stored[s], 16)
                    else:
                        at = g * -1 + (G - 1) if way == "left" else g
                        sp.dma_start(one(dst, at).rearrange("g p a b c -> (g p) (a b c)"), o_t[:, s]).then_inc(stored[s], 16)

                load(0, 0, first=True)
                load(1, 1)
                with sp.Fori(1, G // 2 - 1) as i:
                    for s in range(2):
                        store(2 * i + s - 2, s)
                        load(2 * i + s, s)
                for s in range(2):
                    store(G - 4 + s, s)
                    load(G - 2 + s, s, last=s == 1)
                for s in range(2):
                    store(G - 2 + s, s)
                for s in range(2):
                    sp.wait_ge(stored[s], 16 * STORES * (G // 2))

            @block.tensor
            def _(pe):
                def steps(g, start):
                    for k in range(start, 2 * T):
                        for b in range(B):
                            pe.wait_ge(state_done[b], states0 + T * g + k)
                            for shift in range(3):
                                last = nc.tensor.matmul(ps[:, b, 0:LP], w_sb[:, shift],
                                                        state[:, b, (k - 1) % 2, shift:shift + LP],
                                                        start=shift == 0, stop=shift == 2)
                            last.then_inc(conv_done[b], 1)

                pe.wait_ge(params, 16 * n_params)
                steps(0, 1)
                with pe.Fori(1, G // 2) as i:
                    steps(2 * i, 0)

            @block.vector
            def _(v):
                nc.vector.memset(w_sb[:], 0.0)
                nc.vector.memset(b_sb[:], 0.0)
                nc.vector.memset(state[:], 0.0)
                nc.vector.memset(token[:], 0.0)
                nc.vector.memset(o_t[32:64], 0.0).then_inc(cleared, 1)
                v.wait_ge(params, 16 * n_params)

                def arrived(g, s):
                    if norm:
                        v.wait_ge(normed, g + 1)
                    else:
                        v.wait_ge(loaded[s], 8 * LOADS * (g - s) + 16 * LOADS)

                arrived(0, 0)
                for b in range(B):
                    nc.vector.tensor_copy(state[:, b, 0, 1:LP + 1], line(0, 0, b)).then_inc(state_done[b], 1)

                def steps(g, start):
                    for k in range(start, 2 * T):
                        if k % T == 0:
                            arrived(g + k // T, k // T)
                        for b in range(B):
                            v.wait_ge(conv_done[b], convs0 + T * g + k)
                            if start == 0 or k >= 2:
                                v.wait_ge(copied[b], states0 + T * g + k - 1)
                            nc.vector.scalar_tensor_tensor(state[:, b, k % 2, 1:LP + 1], ps[:, b, 0:LP], b_sb[:, 0:1],
                                                           line(k // T, k % T, b), ALU.add, ALU.add).then_inc(state_done[b], 1)

                steps(0, 1)
                with v.Fori(1, G // 2) as i:
                    steps(2 * i, 0)

            @block.gpsimd
            def _(pool):
                if not norm:
                    return

                def norm_group(g, s, n_in):
                    pool.wait_ge(loaded[s], n_in)
                    nc.gpsimd.tensor_tensor(token[:, s:s + 1], token[:, 2:3], token[:, 2:3], ALU.add)
                    for k in range(0, T, 4):
                        for b in range(B):
                            lines = u_in[:, s].rearrange("p (t b n) -> p t b n", b=B, t=T)[:, k:k + 4, b]
                            ins = nc.gpsimd.tensor_scalar(lines, lines, scale1[:, b:b + 1], bias1[:, b:b + 1],
                                                          ALU.mult, ALU.add)
                    ins.then_inc(normed, 1)

                pool.wait_ge(cleared, 1)
                with pool.Fori(0, G // 2) as i:
                    for s in range(2):
                        norm_group(2 * i + s, s, 16 * i + 16)

            @block.scalar
            def _(act):
                def copy(s, k, b, ph):
                    st = state[:, b, ph, 1:LP + 1]
                    if way in ("down", "right"):
                        return nc.scalar.copy(o_t[:, s].rearrange("p (t b n) -> p t b n", b=B, t=T)[:, k, b], st)
                    if way == "left":
                        return nc.scalar.copy(o_t[:, s].rearrange("p (b n t) -> p b n t", b=B, t=T)[:, b, :, T - 1 - k], st)
                    r, h = (T - 1 - k) % 2, (T - 1 - k) // 2
                    tile = o_t[:, s].rearrange("p (b c h m q) -> p b c h m q", b=B, c=W // T, h=NP, q=2)
                    for q in range(2):
                        ins = nc.scalar.copy(tile[ODD * r:ODD * r + C, b, :, h, :, q],
                                             st[ODD * q:ODD * q + C].rearrange("p (c m) -> p c m", c=W // T))
                    return ins

                def steps(g, first):
                    for k in range(2 * T):
                        s = k // T
                        if k % T == 0 and not first:
                            act.wait_ge(stored[s], 8 * STORES * g)
                        for b in range(B):
                            act.wait_ge(state_done[b], states0 + T * g + k + 1)
                            copy(s, k % T, b, k % 2).then_inc(copied[b], 1)

                act.wait_ge(cleared, 1)
                steps(0, True)
                with act.Fori(1, G // 2) as i:
                    steps(2 * i, False)


def final_sum(nc, sem, x1_rows, l_cols, out):
    with ExitStack() as ctx:
        def sb(name, shape):
            return ctx.enter_context(nc.sbuf_tensor(name, shape, F32))

        res = sb("fin_res", [PP, 2, NP, W])
        lt = sb("fin_l", [PP, 2, G, NP, T])
        o_t = sb("fin_out", [PP, 2, NP, W])
        landed = [sem("fin_in0"), sem("fin_in1")]
        added = sem("fin_added")
        stored = [sem("fin_stored0"), sem("fin_stored1")]
        with nc.Block() as block:
            @block.sync
            def _(sp):
                def load(g, b):
                    sp.dma_start(res[:, b], x1_rows[b, bass.ds(g, 1)].rearrange("g p h w -> (g p) h w")).then_inc(landed[b], 16)
                    sp.dma_start(lt[:, b].rearrange("p c h t -> p c (h t)"),
                                 l_cols[:, :, b, bass.ds(NP * g, NP)].rearrange("c p h t -> p c (h t)")).then_inc(landed[b], 16)

                for b in range(B):
                    load(0, b)
                with sp.Fori(1, G) as g:
                    for b in range(B):
                        sp.wait_ge(added, 2 * g - 1 + b)
                        load(g, b)

            @block.vector
            def _(v):
                def group(g, first):
                    for b in range(B):
                        v.wait_ge(landed[b], 32 * g + 32)
                        if not first:
                            v.wait_ge(stored[b], 32 * g)
                        nc.vector.tensor_tensor(o_t[:, b].rearrange("p h (c t) -> p h c t", t=T),
                                                res[:, b].rearrange("p h (c t) -> p h c t", t=T),
                                                lt[:, b].rearrange("p c h t -> p h c t"), ALU.add).then_inc(added, 1)

                group(0, True)
                with v.Fori(1, G) as g:
                    group(g, False)

            @block.scalar
            def _(act):
                with act.Fori(0, G) as g:
                    for b in range(B):
                        act.wait_ge(added, 2 * g + b + 1)
                        dst = out[b].rearrange("c (m two) w -> two c m w", two=2)
                        for r in range(2):
                            act.dma_start(dst[r, :, bass.ds(NP * g, NP)], o_t[ODD * r:ODD * r + C, b]).then_inc(stored[b], 16)
                for b in range(B):
                    act.wait_ge(stored[b], 32 * G)


def constants():
    import numpy as np
    c = np.arange(B * C)
    same = (c[:, None] // GROUP == c[None, :] // GROUP).astype(np.float32) / np.float32(GROUP)
    gsel = np.zeros((B * C, B, PP), np.float32)
    g112 = np.zeros((PP, PP), np.float32)
    own = same[:C, :C]
    for r in range(2):
        for b in range(B):
            gsel[b * C:(b + 1) * C, b, ODD * r:ODD * r + C] = own
        for q in range(2):
            g112[ODD * r:ODD * r + C, ODD * q:ODD * q + C] = own / 2
    return {"g96": same, "gsel": gsel, "g112": g112, "ident": np.eye(TOK, dtype=np.float32)}


def kernel(**inputs):
    import numpy as np
    import concourse.bacc as bacc
    from concourse.bass_utils import run_bass_kernel_spmd as run

    a = {k: np.asarray(v) for k, v in inputs.items()}
    qkv = a["L0_conv_qkv_w"].reshape(3, HEADS, HC, C)
    dw = a["L0_conv_dw_w"].reshape(3, HEADS, HC, 3, 3)[..., ::-1]
    arrays = {
        "x": a["x"],
        "wqkv": np.concatenate([qkv[:2].transpose(3, 1, 0, 2).reshape(C, 2 * C), qkv[2].reshape(C, C).T], 1),
        "dwqkv": np.concatenate([dw[:2].transpose(3, 4, 1, 0, 2).reshape(3, 3, 2 * C),
                                 dw[2].transpose(2, 3, 0, 1).reshape(3, 3, C)], 2),
        "projT": a["L0_conv_proj_w"].reshape(C, C).T,
        "temp": a["L0_conv_temperature"].reshape(1, HEADS),
    }
    for way in ("down", "right", "left"):
        arrays[f"{way}_w"] = a[f"L1_conv_{way}_w"].transpose(2, 1, 0)
        arrays[f"{way}_b"] = a[f"L1_conv_{way}_b"].reshape(C, 1)
    arrays.update(constants())
    arrays = {k: np.ascontiguousarray(v) for k, v in arrays.items()}

    nc = bacc.Bacc("TRN2", target_bir_lowering=False, num_devices=1)
    args = {k: nc.dram_tensor(k, v.shape, mybir.dt.from_np(v.dtype), kind="ExternalInput").ap() for k, v in arrays.items()}
    out = nc.dram_tensor("out", (B, C, H, W), F32, kind="ExternalOutput").ap()
    program(nc, out=out, **args)
    r = run(nc, [arrays], core_ids=[0])
    return r.results[0]["out"]
```
